# Optimizing a Trainium2 kernel written in Bass

```python
import numpy as np
import jax
import jax.numpy as jnp

def _softmax(x, axis=-1):
    return jax.nn.softmax(x, axis=axis)

def _gelu(x):
    return jax.nn.gelu(x, approximate=True)

def _silu(x):
    return jax.nn.silu(x)

def _sigmoid(x):
    return jax.nn.sigmoid(x)

def _layernorm(x, axis=-1, eps=1e-05):
    m = jnp.mean(x, axis=axis, keepdims=True)
    v = jnp.var(x, axis=axis, keepdims=True)
    return (x - m) / jnp.sqrt(v + eps)

def _scatter_add(tgt, idx, src, axis=0):
    return tgt.at[idx].add(src)

def _segment_sum(src, seg, n):
    return jax.ops.segment_sum(src, seg, n)
kernel_name = 'mk_gnn_preln_d2_gnn_r8_7bb3ac'

def setup_inputs(seed: int=0):
    np.random.seed(seed)
    _w = jnp.asarray

    def _rec_inputs():
        import jax
        import jax.numpy as jnp
        _gk = jax.random.key(seed)
        x = -0.000202 + 1 * jax.random.normal(jax.random.fold_in(_gk, 1), (6250, 64), jnp.float32)
        src = jax.random.randint(jax.random.fold_in(_gk, 2), (200000,), 0, 6250, jnp.int32)
        dst = jax.random.randint(jax.random.fold_in(_gk, 3), (200000,), 0, 6250, jnp.int32)
        _o = jnp.argsort(dst, stable=True)
        src = src[_o]
        dst = dst[_o]
        return (x, src, dst)
    x, src, dst = _rec_inputs()

    def _L0_gnn_setup():
        import jax, jax.numpy as jnp
        import numpy as np
        key = jax.random.key(seed)
        k1, k2, k3 = jax.random.split(key, 3)
        N, E, D = (12500, 156250, 64)
        feat = jax.random.normal(k1, (N, D), dtype=jnp.float32)
        src = jax.random.randint(k2, (E,), 0, N, dtype=jnp.int32)
        dst = jax.random.randint(k3, (E,), 0, N, dtype=jnp.int32)
        return {'feat': feat, 'src': src, 'dst': dst, 'n_nodes': N}
    _L0_gnn_all = _L0_gnn_setup()
    _L0_gnn_in = {k: v for k, v in _L0_gnn_all.items() if k in ()}
    del _L0_gnn_all

    def _L1_gnn_setup():
        import jax, jax.numpy as jnp
        import numpy as np
        N_NODES = 12500
        N_EDGES = 150000
        HID = 64
        N_LAYERS = 3
        GAMMA = -0.45
        ZETA = 1.05
        key = jax.random.key(seed)
        ks = jax.random.split(key, 8)
        s = 0.05
        return {'features': jax.random.normal(ks[0], (N_NODES, HID), jnp.float32), 'nb_W': jax.random.normal(ks[1], (N_LAYERS, HID, HID), jnp.float32) * s, 'nb_b': jnp.zeros((N_LAYERS, HID), jnp.float32), 'self_W': jax.random.normal(ks[2], (N_LAYERS, HID, HID), jnp.float32) * s, 'self_b': jnp.zeros((N_LAYERS, HID), jnp.float32), 'att1_W': jax.random.normal(ks[3], (N_LAYERS, 2 * HID, HID), jnp.float32) * s, 'att1_b': jnp.zeros((N_LAYERS, HID), jnp.float32), 'att2_W': jax.random.normal(ks[4], (N_LAYERS, HID, 1), jnp.float32) * s, 'att2_b': jnp.zeros((N_LAYERS, 1), jnp.float32), 'row': jax.random.randint(ks[5], (N_EDGES,), 0, N_NODES, jnp.int32), 'col': jax.random.randint(ks[6], (N_EDGES,), 0, N_NODES, jnp.int32)}
    _L1_gnn_all = _L1_gnn_setup()
    _L1_gnn_in = {k: v for k, v in _L1_gnn_all.items() if k in ('nb_W', 'nb_b', 'self_W', 'self_b', 'att1_W', 'att1_b', 'att2_W', 'att2_b')}
    del _L1_gnn_all
    return {'x': x, 'src': src, 'dst': dst, 'L1_gnn_nb_W': _L1_gnn_in['nb_W'], 'L1_gnn_nb_b': _L1_gnn_in['nb_b'], 'L1_gnn_self_W': _L1_gnn_in['self_W'], 'L1_gnn_self_b': _L1_gnn_in['self_b'], 'L1_gnn_att1_W': _L1_gnn_in['att1_W'], 'L1_gnn_att1_b': _L1_gnn_in['att1_b'], 'L1_gnn_att2_W': _L1_gnn_in['att2_W'], 'L1_gnn_att2_b': _L1_gnn_in['att2_b']}

def reference(x, src, dst, L1_gnn_nb_W, L1_gnn_nb_b, L1_gnn_self_W, L1_gnn_self_b, L1_gnn_att1_W, L1_gnn_att1_b, L1_gnn_att2_W, L1_gnn_att2_b):
    import jax
    import jax.numpy as jnp

    def _L0_gnn_ref(feat, src, dst, n_nodes):
        import jax, jax.numpy as jnp
        import numpy as np
        messages = feat[src]
        out = jax.ops.segment_sum(messages, dst, num_segments=n_nodes)
        return out

    def _L1_gnn_ref(features, nb_W, nb_b, self_W, self_b, att1_W, att1_b, att2_W, att2_b, row, col):
        import jax, jax.numpy as jnp
        import numpy as np
        N_NODES = 12500
        N_EDGES = 150000
        HID = 64
        N_LAYERS = 3
        GAMMA = -0.45
        ZETA = 1.05
        n = features.shape[0]
        x = features
        out = features
        for l in range(N_LAYERS):
            f1 = jax.nn.relu(x[row] @ nb_W[l] + nb_b[l])
            f2 = jax.nn.relu(x[col] @ self_W[l] + self_b[l])
            h = jax.nn.relu(jnp.concatenate([f1, f2], axis=1) @ att1_W[l] + att1_b[l])
            log_alpha = (h @ att2_W[l] + att2_b[l])[:, 0]
            mask = jnp.clip(jax.nn.sigmoid(log_alpha) * (ZETA - GAMMA) + GAMMA, 0.0, 1.0)
            rowsum = jax.ops.segment_sum(mask, row, num_segments=n) + 1e-06
            d_inv_sqrt = jnp.clip(rowsum ** (-0.5), 0.0, 10.0)
            vals = mask * d_inv_sqrt[row] * d_inv_sqrt[col]
            x = jax.ops.segment_sum(vals[:, None] * x[col], row, num_segments=n)
            out = out + x
        return out
    h = jnp.maximum(_layernorm(x, axis=-1), 0.0)
    x = x + _L0_gnn_ref(h, src, dst, 6250)
    h = jnp.maximum(_layernorm(x, axis=-1), 0.0)
    x = x + _L1_gnn_ref(h, L1_gnn_nb_W, L1_gnn_nb_b, L1_gnn_self_W, L1_gnn_self_b, L1_gnn_att1_W, L1_gnn_att1_b, L1_gnn_att2_W, L1_gnn_att2_b, src, dst)
    return x

_drawn_inputs = setup_inputs


def setup_inputs(seed=0):
    import zlib

    import numpy as np

    out = dict(_drawn_inputs(seed))
    spreads = {'L1_gnn_nb_b': (0.0, 0.8),
     'L1_gnn_self_b': (0.0, 0.8),
     'L1_gnn_att1_b': (0.0, 0.8),
     'L1_gnn_att2_b': (0.0, 0.8)}
    factors = {'L1_gnn_nb_W': 8.0, 'L1_gnn_self_W': 8.0, 'L1_gnn_att1_W': 8.0, 'L1_gnn_att2_W': 8.0}
    for name, (base, spread) in spreads.items():
        noise = np.random.default_rng([zlib.crc32(name.encode()), seed]).standard_normal(out[name].shape)
        drawn = base * np.exp(spread * noise) if base else spread * noise
        out[name] = jnp.asarray(drawn.astype(out[name].dtype))
    for name, factor in factors.items():
        out[name] = (out[name] * factor).astype(out[name].dtype)
    return out
```

```python
import concourse.bass as bass
from concourse import mybir
from contextlib import ExitStack, contextmanager

F32 = mybir.dt.float32
F16 = mybir.dt.float16
BF16 = mybir.dt.bfloat16
FP8 = mybir.dt.float8e4
I32 = mybir.dt.int32
U8 = mybir.dt.uint8
ALU = mybir.AluOpType
ACT = mybir.ActivationFunctionType
X = mybir.AxisListType.X

P = 128
PARTS = 3
CH = 8
HOT = 56
GAMMA, ZETA = -0.45, 1.05
EPS_LN, EPS_SUM, D_MAX = 1e-5, 1e-6, 10.0



class Record:
    pass


class Chain:

    def __init__(self, eng, sem, base=0):
        self.eng, self.sem, self.base, self.n = eng, sem, base, 0

    def __call__(self, ins):
        ins.then_inc(self.sem, 1)
        self.n += 1
        self.eng.wait_ge(self.sem, self.base + self.n)


def wait_count(eng, s, sem, value):
    eng.wait_ge(sem, value)
    if not isinstance(value, int):
        eng.sem_inc(s["passed"], 1)


def carry_waits(nc, k, spare):
    nc.tensor.matmul(spare, k.zero[:, :], k.zero[:, 0:1], start=True, stop=True)


@contextmanager
def phase(nc, names, again=False):
    with ExitStack() as st:
        sems = {n: st.enter_context(nc.semaphore(n)) for n in names.split()}
        with nc.Block() as block:
            yield sems, block
        if again:
            zero(nc, sems)


def zero(nc, sems):
    numbers = [h.num for h in sems.values()]
    assert max(numbers) - min(numbers) + 1 == len(numbers)
    nc.gpsimd.sem_clear(range(min(numbers), max(numbers) + 1))


@contextmanager
def spill_phase(nc, k):
    with nc.Block() as block:
        yield k.spill_sems, block
    numbers = [h.num for h in k.spill_sems.values()]
    nc.gpsimd.dma_reset(range(min(numbers), max(numbers) + 1))
    zero(nc, k.spill_sems)
    nc.all_engine_barrier()


def each_row(eng, nb, row):
    row(0, 0, 1, True)
    with eng.Fori(0, (nb - 1) // 2) as i:
        row(i * 2 + 1, 1, i + 1, False)
        row(i * 2 + 2, 0, i + 2, False)


def make_plan(x, src, dst, nb_w, out, cap):
    k = Record()
    k.N, k.D = x.shape
    k.E = src.shape[0]
    k.L = nb_w.shape[0]
    k.NB = -(-k.N // P)
    assert k.NB % 2 == 1 and k.D == 64
    k.G = max(g for g in range(1, 8) if k.NB % g == 0)
    k.NG = k.NB // k.G
    k.NT = -(-k.E // (P * 2 * CH)) * 2 * CH
    k.NTP = k.NT + CH
    k.SLOTS = k.NB * k.NB * P
    k.PAD = k.NB * P
    k.MID = k.NB * k.NB // 2
    assert k.NB * k.NB + k.NB - k.MID < 2048
    k.CAP = cap
    return k


def allocate(nc, k, st):
    def sb(name, shape, dt):
        return st.enter_context(nc.sbuf_tensor(name, shape, dt))

    k.iota = sb("iota", [P, P], F32)
    k.pcol = sb("pcol", [P, 1], F32)
    k.ident = sb("ident", [P, P], F32)
    k.ident16 = sb("ident16", [P, P], F16)
    k.identb = sb("identb", [P, P], BF16)
    k.before = sb("before", [P, P], BF16)
    k.ones = sb("ones", [P, P], F32)
    k.zero = sb("zero", [P, P], BF16)
    k.srci = sb("srci", [P, k.NTP], I32)
    k.dsti = sb("dsti", [P, k.NTP], I32)
    k.spill = sb("spill", [P, k.NT], F32)
    k.res = sb("res", [P, k.NB * k.D], F32)
    k.cur = sb("cur", [P, k.NB * k.D], F32)
    k.one = sb("one", [P, k.NB * k.D], F32)
    k.two = sb("two", [P, k.NB * k.D], F32)
    k.table_s = sb("table_s", [P, k.NB, PARTS, k.D], BF16)
    k.table_d = sb("table_d", [P, k.NB, PARTS, k.D], BF16)
    k.mean = sb("mean", [P, k.NB], F32)
    k.var = sb("var", [P, k.NB], F32)
    k.root = sb("root", [P, k.NB], F32)
    k.inv = sb("inv", [P, k.NB], F32)
    k.col_spills = sb("col_spills", [1, k.NT], I32)
    k.some_spill = sb("some_spill", [1, 1], I32)
    k.spill_mask = sb("spill_mask", [P, k.NT], F32)
    names = "spill_stored picked gathered_rows placed multiplied step"
    k.spill_sems = {n: st.enter_context(nc.semaphore("spill_" + n)) for n in names.split()}


def allocate_sort(nc, k, st):
    def sb(name, shape, dt):
        return st.enter_context(nc.sbuf_tensor(name, shape, dt))

    k.itmp = sb("itmp", [P, k.NTP], I32)
    k.bs = sb("bs", [P, k.NTP], F32)
    k.bd = sb("bd", [P, k.NTP], F32)
    k.place = sb("place", [P, k.NTP, 2], BF16)
    k.key = sb("key", [P, k.NTP], F32)
    k.key16 = sb("key16", [P, k.NTP], F16)
    k.empty = sb("empty", [P, -(-k.SLOTS // (2 * P)) * 2 + 2], BF16)


def constants(nc, k):
    with phase(nc, "iota_done made") as (s, block):
        @block.gpsimd
        def _(pool):
            nc.gpsimd.iota(k.iota[:, :], [[1, P]], base=0, channel_multiplier=0,
                           allow_small_or_imprecise_dtypes=True).then_inc(s["iota_done"], 1)
            nc.gpsimd.iota(k.pcol[:, :], [[0, 1]], base=0, channel_multiplier=1,
                           allow_small_or_imprecise_dtypes=True).then_inc(s["iota_done"], 1)

        @block.vector
        def _(dve):
            dve.wait_ge(s["iota_done"], 2)
            for t in (k.ident, k.ident16, k.identb):
                nc.vector.tensor_scalar(t[:, :], k.iota[:, :], k.pcol[:, 0:1], None, ALU.is_equal)
            nc.vector.tensor_scalar(k.before[:, :], k.iota[:, :], k.pcol[:, 0:1], None, ALU.is_lt)
            nc.vector.memset(k.ones[:, :], 1.0)
            nc.vector.memset(k.zero[:, :], 0.0).then_inc(s["made"], 1)
            dve.wait_ge(s["made"], 1)


def load_edges(nc, k, src, dst):
    full, rest = k.E // k.NT, k.E % k.NT
    cuts = [c for c in (0, full // 16 * 16, full) if c <= full]
    spans = [(a, b) for a, b in zip(cuts, cuts[1:]) if b > a]
    n_loads = 2 * (len(spans) + (rest > 0))
    with phase(nc, "padded loaded step") as (s, block):
        @block.sync
        def _(sp):
            sp.wait_ge(s["padded"], 2)
            for e, t in ((src, k.srci), (dst, k.dsti)):
                for a, b in spans:
                    sp.dma_start(t[a:b, 0:k.NT],
                                 e[a * k.NT:b * k.NT].rearrange("(p t) -> p t", t=k.NT)).then_inc(s["loaded"], 16)
                if rest:
                    sp.dma_start(t[full:full + 1, 0:rest],
                                 e[full * k.NT:k.E].rearrange("(p t) -> p t", p=1)).then_inc(s["loaded"], 16)

        @block.vector
        def _(dve):
            step = Chain(dve, s["step"])
            nc.vector.memset(k.srci[:, :], k.PAD).then_inc(s["padded"], 1)
            nc.vector.memset(k.dsti[:, :], k.PAD).then_inc(s["padded"], 1)
            dve.wait_ge(s["padded"], 2)
            dve.wait_ge(s["loaded"], 16 * n_loads)
            for n, (ends, blk) in enumerate(((k.srci, k.bs), (k.dsti, k.bd))):
                step(nc.vector.tensor_single_scalar(k.itmp[:, :], ends[:, :], 7, ALU.logical_shift_right))
                step(nc.vector.tensor_copy(blk[:, :], k.itmp[:, :]))
                step(nc.vector.tensor_single_scalar(k.itmp[:, :], ends[:, :], P - 1, ALU.bitwise_and))
                step(nc.vector.tensor_copy(k.place[:, :, n], k.itmp[:, :]))
            step(nc.vector.scalar_tensor_tensor(k.key[:, :], k.bs[:, :], float(k.NB), k.bd[:, :], ALU.mult, ALU.add))
            step(nc.vector.tensor_scalar(k.key16[:, :], k.key[:, :], float(-k.MID), None, ALU.add))
            step(nc.vector.memset(k.empty[:, :], -1.0))


def sort_edges(nc, k):
    NB, NPAIR = k.NB, k.NT // (2 * CH)
    with ExitStack() as st:
        def sb(name, shape, dt):
            return st.enter_context(nc.sbuf_tensor(name, shape, dt))

        def ps(name, shape, dt=F32):
            return st.enter_context(nc.psum_tensor(name, shape, dt))

        key_st = sb("key_st", [P, 2, CH], F16)
        one_s = sb("one_s", [P, 2, CH, NB], BF16)
        one_d = sb("one_d", [P, 2, CH, NB], BF16)
        one_sT = sb("one_sT", [NB, CH, P], F32)
        count_sb = sb("count_sb", [NB, 2, NB], F32)
        same = sb("same", [P, CH, P], BF16)
        picked = sb("picked", [P, CH, NB], F32)
        before_col = sb("before_col", [P, CH], F32)
        in_col = sb("in_col", [P, 2, CH], F32)
        rank = sb("rank", [P, CH], F32)
        over = sb("over", [P, CH], F32)
        slot_f = sb("slot_f", [P, CH], F32)
        slot = sb("slot", [P, 2, CH], I32)
        place_st = sb("place_st", [P, 2, CH, 2], BF16)
        rows_ps = [ps(f"rows_ps{i}", [P, CH, P]) for i in range(2)]
        one_sT_ps = ps("one_sT_ps", [NB, CH, P], BF16)
        before_ps = [ps(f"before_ps{i}", [P, CH, NB]) for i in range(2)]
        count_ps = ps("count_ps", [NB, NB])

        with phase(nc, "passed init_a init_b staged rows transposed one_sT_ready counted count_ready ranked slots_ready "
                       "step") as (s, block):
            scattered = [s["init_a"], s["init_b"]]

            @block.gpsimd
            def _(pool):
                for h in range(2):
                    lo, hi = (0, k.NB * k.NB // 2 * P) if h == 0 else (k.NB * k.NB // 2 * P, k.SLOTS)
                    pool.dma_start(k.slots_dram[lo:hi, :].rearrange("(p a) b -> p (a b)", p=P),
                                   k.empty[:, 0:(hi - lo) // P * 2]).then_inc(scattered[h], 16)
                for h in range(2):
                    pool.wait_ge(scattered[h], 16)
                with pool.Fori(0, NPAIR) as i:
                    for b in range(2):
                        wait_count(pool, s, s["slots_ready"], i * 2 + b + 1)
                        for j in range(CH):
                            nc.gpsimd.indirect_dma_start(
                                out=k.slots_dram[:, :],
                                out_offset=bass.IndirectOffsetOnAxis(ap=slot[:, b, j:j + 1], axis=0),
                                in_=place_st[:, b, j, :], in_offset=None,
                                bounds_check=k.SLOTS - 1, oob_is_err=False).then_inc(scattered[b], 16)
                for h in range(2):
                    pool.wait_ge(scattered[h], 16 + 16 * CH * NPAIR)

            @block.tensor
            def _(pe):
                nc.tensor.matmul(count_ps[:, :], k.zero[:, 0:NB], k.zero[:, 0:NB], start=True, stop=False,
                                 skip_group_check=True).then_inc(s["counted"], 1)
                with pe.Fori(0, NPAIR) as i:
                    for b in range(2):
                        chunk = i * 2 + b
                        pe.wait_ge(s["staged"], chunk + 1)
                        for j in range(CH):
                            last = nc.tensor.matmul(rows_ps[b][:, j, :], key_st[:, b, j:j + 1].to_broadcast([P, P]),
                                                    k.ident16[:, :], start=True, stop=True)
                        last.then_inc(s["rows"], 1)
                        for j in range(CH):
                            last = nc.tensor.transpose(one_sT_ps[:, j, :], one_s[:, b, j, :], k.identb[:, :])
                        last.then_inc(s["transposed"], 1)
                        pe.wait_ge(s["one_sT_ready"], chunk + 1)
                        for j in range(CH):
                            t = i * (2 * CH) + b * CH + j
                            pe.wait_ge(s["count_ready"], t + 1)
                            nc.tensor.matmul(count_ps[:, :], one_s[:, b, j, :], one_d[:, b, j, :],
                                             start=False, stop=False, skip_group_check=True).then_inc(s["counted"], 1)
                            last = nc.tensor.matmul(before_ps[b][:, j, :], one_sT[:, j, :],
                                                    count_sb[:, j % 2, :], start=True, stop=True)
                        last.then_inc(s["ranked"], 1)

            @block.scalar
            def _(act):
                act.wait_ge(s["counted"], 1)
                nc.scalar.activation(count_sb[:, 0, :], count_ps[:, :], ACT.Copy).then_inc(s["count_ready"], 1)
                with act.Fori(0, NPAIR) as i:
                    for b in range(2):
                        act.wait_ge(s["transposed"], i * 2 + b + 1)
                        nc.scalar.activation(one_sT[:, :, :], one_sT_ps[:, :, :], ACT.Copy).then_inc(s["one_sT_ready"], 1)
                        for j in range(CH):
                            act.wait_ge(s["counted"], i * (2 * CH) + b * CH + j + 2)
                            nc.scalar.activation(count_sb[:, (j + 1) % 2, :], count_ps[:, :],
                                                 ACT.Copy).then_inc(s["count_ready"], 1)

            @block.vector
            def _(dve):
                def stage(chunk, b):
                    at = bass.ds(chunk * CH, CH)
                    nc.vector.tensor_copy(key_st[:, b, :], k.key16[:, at])
                    for one, blk in ((one_s, k.bs), (one_d, k.bd)):
                        last = nc.vector.tensor_tensor(
                            one[:, b, :, :], k.iota[:, 0:NB].unsqueeze(1).to_broadcast([P, CH, NB]),
                            blk[:, at].unsqueeze(2).to_broadcast([P, CH, NB]), ALU.is_equal)
                    last.then_inc(s["staged"], 1)

                stage(0, 0)
                with dve.Fori(0, NPAIR) as i:
                    for b in range(2):
                        chunk = i * 2 + b
                        at = bass.ds(chunk * CH, CH)
                        stage(chunk + 1, 1 - b)
                        step = Chain(dve, s["step"], chunk * 5)
                        dve.wait_ge(s["rows"], chunk + 1)
                        for j in range(CH):
                            last = nc.vector.scalar_tensor_tensor(
                                same[:, j, :], rows_ps[b][:, j, :], key_st[:, b, j:j + 1], k.before[:, :],
                                ALU.is_equal, ALU.mult, accum_out=in_col[:, b, j:j + 1])
                        step(last)
                        dve.wait_ge(s["ranked"], chunk + 1)
                        step(nc.vector.tensor_tensor(picked[:, :, :], before_ps[b][:, :, :], one_d[:, b, :, :], ALU.mult))
                        step(nc.vector.tensor_reduce(before_col[:, :], picked[:, :, :], X, ALU.add))
                        step(nc.vector.tensor_tensor(rank[:, :], before_col[:, :], in_col[:, b, :], ALU.add))
                        nc.vector.tensor_scalar(k.spill[:, at], rank[:, :], float(k.CAP), None, ALU.is_ge)
                        nc.vector.tensor_scalar(over[:, :], rank[:, :], float(k.CAP), float(2 * k.SLOTS),
                                                ALU.is_ge, ALU.mult)
                        step(nc.vector.scalar_tensor_tensor(slot_f[:, :], k.key[:, at], float(P), rank[:, :],
                                                            ALU.mult, ALU.add))
                        dve.wait_ge(scattered[b], i * (16 * CH) + 16)
                        nc.vector.tensor_copy(place_st[:, b, :, :], k.place[:, at, :])
                        nc.vector.tensor_tensor(slot[:, b, :], slot_f[:, :], over[:, :], ALU.add)\
                            .then_inc(s["slots_ready"], 1)



def nodes(k, t):
    return t[:, :].rearrange("p (b d) -> p b d", d=k.D)


def split3(k, step, table, rows, rest):
    step(step.eng.tensor_copy(table[:, :, 0, :], rows))
    step(step.eng.tensor_tensor(rest, rows, table[:, :, 0, :], ALU.subtract))
    step(step.eng.tensor_copy(table[:, :, 1, :], rest))
    step(step.eng.tensor_tensor(rest, rest, table[:, :, 1, :], ALU.subtract))
    step(step.eng.tensor_copy(table[:, :, 2, :], rest))


def inverse_root(s, step, value, root, inv, tmp):
    dve = step.eng
    dve.wait_ge(s["root_ready"], 1)
    step(dve.reciprocal(inv, root))
    step(dve.tensor_tensor(tmp, inv, inv, ALU.mult))
    step(dve.tensor_tensor(tmp, tmp, value, ALU.mult))
    step(dve.tensor_scalar(tmp, tmp, -0.5, 1.5, ALU.mult, ALU.add))
    step(dve.tensor_tensor(inv, inv, tmp, ALU.mult))


def normalise(k, s, step, rows, h, centred):
    dve = step.eng
    shape = [P, k.NB, k.D]

    def wide(t):
        return t[:, :].unsqueeze(2).to_broadcast(shape)

    step(dve.tensor_reduce(k.mean[:, :], rows, X, ALU.add))
    step(dve.tensor_scalar(k.mean[:, :], k.mean[:, :], 1.0 / k.D, None, ALU.mult))
    step(dve.tensor_tensor(centred, rows, wide(k.mean), ALU.subtract))
    step(dve.tensor_tensor(h, centred, centred, ALU.mult))
    step(dve.tensor_reduce(k.var[:, :], h, X, ALU.add))
    dve.tensor_scalar(k.var[:, :], k.var[:, :], 1.0 / k.D, EPS_LN, ALU.mult, ALU.add).then_inc(s["value_ready"], 1)
    inverse_root(s, step, k.var[:, :], k.root[:, :], k.inv[:, :], k.mean[:, :])
    step(dve.tensor_tensor(centred, centred, wide(k.inv), ALU.mult))
    step(dve.tensor_scalar(h, centred, 0.0, None, ALU.max))


def sqrt_on_act(nc, k, s):
    def program(act):
        act.wait_ge(s["value_ready"], 1)
        nc.scalar.activation(k.root[:, :], k.var[:, :], ACT.Sqrt).then_inc(s["root_ready"], 1)
    return program


def idle(eng):
    pass


def count_spills(nc, k):
    spans = [(a, min(a + 512, k.NT)) for a in range(0, k.NT, 512)]
    with ExitStack() as st:
        col_ps = [st.enter_context(nc.psum_tensor(f"col_ps{i}", [P, 512], F32)) for i in range(len(spans))]
        all_f = st.enter_context(nc.sbuf_tensor("all_f", [1, len(spans)], F32))
        with phase(nc, "summed step") as (s, block):
            @block.tensor
            def _(pe):
                for i, (a, z) in enumerate(spans):
                    last = nc.tensor.matmul(col_ps[i][:, 0:z - a], k.ones[:, :], k.spill[:, a:z], start=True, stop=True)
                last.then_inc(s["summed"], 1)

            @block.vector
            def _(dve):
                step = Chain(dve, s["step"])
                dve.wait_ge(s["summed"], 1)
                for i, (a, z) in enumerate(spans):
                    dve.tensor_copy(k.col_spills[:, a:z], col_ps[i][0:1, 0:z - a])
                    last = dve.tensor_reduce(all_f[:, i:i + 1], col_ps[i][0:1, 0:z - a], X, ALU.add)
                step(last)
                with nc.allow_low_precision("whole numbers"):
                    step(dve.tensor_reduce(k.some_spill[:, :], all_f[:, :], X, ALU.max))


def spilled_edges(nc, k, stored, gathers, by, acc, width, stage):
    NB, D = k.NB, k.D
    group = max(g for g in range(1, NB + 1) if NB % g == 0 and g * width <= 512)
    n = NB // group
    spilled = nc.values_load(k.some_spill[0:1, 0:1], skip_runtime_bounds_check_because="only tested")
    with nc.If(spilled > 0):
        with spill_phase(nc, k) as (s, block):
            @block.sync
            def _(sp):
                for rows, table in stored:
                    sp.dma_start(table.rearrange("(b p) d -> p b d", p=P), nodes(k, rows)).then_inc(s["spill_stored"], 16)
                sp.wait_ge(s["spill_stored"], 16 * len(stored))

            for engine in (block.gpsimd, block.tensor, block.scalar, block.vector):
                engine(idle)
        with nc.Fori(0, k.NT) as t:
            in_col = nc.values_load(k.col_spills[0:1, bass.ds(t, 1)], skip_runtime_bounds_check_because="only tested")
            with nc.If(in_col > 0):
                spilled_column(nc, k, t, gathers, by, acc, width, stage, group, n)
        nc.all_engine_barrier()


def spilled_column(nc, k, t, gathers, by, acc, width, stage, group, n):
    NB, D = k.NB, k.D
    with ExitStack() as st:
        def sb(name, shape, dt):
            return st.enter_context(nc.sbuf_tensor(name + "_" + stage, shape, dt))

        index = sb("sp_index", [P, 2], I32)
        ends = sb("sp_ends", [P, 2], I32)
        ends_f = sb("sp_ends_f", [P, 2], F32)
        place = sb("sp_place", [P, P], F32)
        block_hot = sb("sp_block", [P, NB], F32)
        row = sb("sp_row", [P, 2, D], F32)
        logit = sb("sp_logit", [P, 1], F32)
        spread = nodes(k, k.two) if width > 1 else sb("sp_spread", [P, NB, 1], F32)
        total_ps = [st.enter_context(nc.psum_tensor(f"sp_ps{i}_{stage}", [P, group, width], F32)) for i in range(n)]
        with spill_phase(nc, k) as (s, block):
            block.sync(idle)

            @block.gpsimd
            def _(pool):
                pool.wait_ge(s["picked"], 1)
                for i, (table, _e) in enumerate(gathers):
                    pool.indirect_dma_start(out=row[:, i, :], out_offset=None, in_=table,
                                            in_offset=bass.IndirectOffsetOnAxis(ap=index[:, i:i + 1], axis=0),
                                            bounds_check=NB * P - 1, oob_is_err=False).then_inc(s["gathered_rows"], 16)

            @block.tensor
            def _(pe):
                pe.wait_ge(s["placed"], 1)
                for i in range(n):
                    last = pe.matmul(total_ps[i][:, :, :], place[:, :], spread[:, i * group:(i + 1) * group, :],
                                     start=True, stop=True)
                last.then_inc(s["multiplied"], 1)

            @block.scalar
            def _(act):
                if stage == "masks":
                    act.wait_ge(s["multiplied"], 1)
                    act.activation(logit[:, :], logit[:, :], ACT.Sigmoid, bias=k.b3[:, 0:1]).then_inc(s["multiplied"], 1)

            @block.vector
            def _(dve):
                step = Chain(dve, s["step"])
                edge = bass.ds(t, 1)
                for i, (_t, end) in enumerate(gathers):
                    last = dve.tensor_single_scalar(index[:, i:i + 1], end[:, edge], NB * P - 1, ALU.min)
                last.then_inc(s["picked"], 1)
                dve.tensor_single_scalar(ends[:, 0:1], by[:, edge], 7, ALU.logical_shift_right)
                step(dve.tensor_single_scalar(ends[:, 1:2], by[:, edge], P - 1, ALU.bitwise_and))
                step(dve.tensor_copy(ends_f[:, :], ends[:, :]))
                dve.tensor_scalar(place[:, :], k.iota[:, :], ends_f[:, 1:2], None, ALU.is_equal)
                step(dve.tensor_scalar(block_hot[:, :], k.iota[:, 0:NB], ends_f[:, 0:1], k.spill[:, edge],
                                       ALU.is_equal, ALU.mult))
                dve.wait_ge(s["gathered_rows"], 16 * len(gathers))
                summed = 1
                if stage == "masks":
                    step(dve.tensor_tensor(row[:, 0, :], row[:, 0, :], row[:, 1, :], ALU.add))
                    step(dve.scalar_tensor_tensor(row[:, 0, :], row[:, 0, :], 0.0, k.w3[:, :], ALU.max, ALU.mult))
                    dve.tensor_reduce(logit[:, :], row[:, 0, :], X, ALU.add).then_inc(s["multiplied"], 1)
                    dve.wait_ge(s["multiplied"], 2)
                    step(dve.tensor_scalar(logit[:, :], logit[:, :], ZETA - GAMMA, GAMMA, ALU.mult, ALU.add))
                    step(dve.tensor_scalar(logit[:, :], logit[:, :], 0.0, 1.0, ALU.max, ALU.min))
                    dve.tensor_copy(k.spill_mask[:, edge], logit[:, :])
                    step(dve.tensor_scalar(spread[:, :, 0], block_hot[:, :], logit[:, 0:1], None, ALU.mult))
                    summed = 3
                else:
                    if stage == "messages":
                        step(dve.tensor_tensor(block_hot[:, :], block_hot[:, :],
                                               k.spill_mask[:, edge].to_broadcast([P, NB]), ALU.mult))
                    step(dve.tensor_tensor(spread[:, :, :], block_hot[:, :].unsqueeze(2).to_broadcast([P, NB, D]),
                                           row[:, 0, :].unsqueeze(1).to_broadcast([P, NB, D]), ALU.mult))
                dve.sem_inc(s["placed"], 1)
                dve.wait_ge(s["multiplied"], summed)
                for i in range(n):
                    part = acc[:, i * group:(i + 1) * group, :]
                    last = dve.tensor_tensor(part, part, total_ps[i][:, :, :], ALU.add)
                step(last)


def first_table(nc, k, x):
    whole = k.N // P
    with phase(nc, "padded loaded value_ready root_ready step") as (s, block):
        @block.sync
        def _(sp):
            sp.wait_ge(s["padded"], 1)
            sp.dma_start(nodes(k, k.res)[:, 0:whole, :],
                         x[0:whole * P, :].rearrange("(b p) d -> p b d", p=P)).then_inc(s["loaded"], 16)
            if k.N > whole * P:
                sp.dma_start(nodes(k, k.res)[0:k.N - whole * P, whole, :], x[whole * P:k.N, :]).then_inc(s["loaded"], 16)

        block.scalar(sqrt_on_act(nc, k, s))

        @block.vector
        def _(dve):
            step = Chain(dve, s["step"])
            dve.memset(k.res[:, :], 0.0).then_inc(s["padded"], 1)
            dve.wait_ge(s["loaded"], 16 * (1 + (k.N > whole * P)))
            normalise(k, s, step, nodes(k, k.res), nodes(k, k.cur), nodes(k, k.one))
            split3(k, step, k.table_s, nodes(k, k.cur), nodes(k, k.one))


def build_and_sum(nc, k):
    NB, G, NG, D = k.NB, k.G, k.NG, k.D
    Q = NB * NG
    with ExitStack() as st:
        def sb(name, shape, dt):
            return st.enter_context(nc.sbuf_tensor(name, shape, dt))

        def ps(name, shape, dt=F32):
            return st.enter_context(nc.psum_tensor(name, shape, dt))

        places = sb("places", [P, NG, G * P, 2], BF16)
        hot = sb("hot", [P, NG, 3, G * P], U8)
        hot_d = sb("hot_d", [P, 2, G, P], U8)
        counts = sb("counts", [P, 2, G, P], BF16)
        rows = sb("rows", [P, 2, PARTS * D], BF16)
        src_ps = ps("src_ps", [P, 8, P])
        dst_ps = ps("dst_ps", [P, 8, P])
        cnt_ps = ps("cnt_ps", [P, 8, P])
        sum_ps = ps("sum_ps", [P, G, D])
        sems = " ".join([f"places_in{g} stored{g}" for g in range(NG)])
        with phase(nc, "passed hotT src_turned dst_turned hot_ready hot_d_ready counted counts_ready "
                       "rows_ready summed added step " + sems) as (s, block):
            places_in = [s[f"places_in{g}"] for g in range(NG)]
            stored = [s[f"stored{g}"] for g in range(NG)]

            @block.gpsimd
            def _(pool):
                def row(r, b, nth, first):
                    for g in range(NG):
                        if not first:
                            wait_count(pool, s, s["hotT"], (r - 1) * NG + g + 1)
                        tile = k.slots_dram[bass.ds((r * NB + g * G) * P, G * P), :]
                        pool.dma_start(places[:, g, :, :], tile.rearrange("a b -> (a b)").partition_broadcast(P))\
                            .then_inc(places_in[g], 16)
                each_row(pool, NB, row)

            @block.sync
            def _(sp):
                def row(r, b, nth, first):
                    for g in range(NG):
                        q = r * NG + g
                        wait_count(sp, s, s["hotT"], q + 1)
                        wait_count(sp, s, s["hot_ready"], q + 1)
                        sp.dma_start(k.hot_dram[bass.ds(r, 1), :, g, :, :].rearrange("r p a b -> (r p) a b"),
                                     hot[:, g, :, :]).then_inc(stored[g], 16)
                each_row(sp, NB, row)
                for g in range(NG):
                    sp.wait_ge(stored[g], 16 * NB)

            @block.tensor
            def _(pe):
                def turn(r, g, first):
                    q = r * NG + g
                    pe.wait_ge(s["hotT"], q + 1)
                    if not (first and g == 0):
                        pe.wait_ge(s["hot_ready"], q)
                    carry_waits(nc, k, src_ps[:, 7, 0:1])
                    for j in range(G):
                        last = nc.tensor.matmul(src_ps[:, j, :], hot[:, g, 0, j * P:(j + 1) * P].bitcast(FP8), k.identb[:, :],
                                                start=True, stop=True)
                    last.then_inc(s["src_turned"], 1)
                    if not (first and g == 0):
                        pe.wait_ge(s["hot_d_ready"], q)
                    carry_waits(nc, k, dst_ps[:, 7, 0:1])
                    for j in range(G):
                        last = nc.tensor.matmul(dst_ps[:, j, :], hot[:, g, 1, j * P:(j + 1) * P].bitcast(FP8), k.identb[:, :],
                                                start=True, stop=True)
                    last.then_inc(s["dst_turned"], 1)

                def count(q, g, b):
                    pe.wait_ge(s["hot_ready"], q + 1)
                    pe.wait_ge(s["hot_d_ready"], q + 1)
                    carry_waits(nc, k, cnt_ps[:, 7, 0:1])
                    for j in range(G):
                        last = nc.tensor.matmul(cnt_ps[:, j, :], hot[:, g, 2, j * P:(j + 1) * P].bitcast(FP8),
                                                hot_d[:, (b + g) % 2, j, :].bitcast(FP8), start=True, stop=True)
                    last.then_inc(s["counted"], 1)

                def add_up(q, r, g, b):
                    pe.wait_ge(s["counts_ready"], q + 1)
                    pe.wait_ge(s["rows_ready"], r + 1)
                    pe.wait_ge(s["added"], q + 1)
                    for j in range(G):
                        for part in range(PARTS):
                            last = nc.tensor.matmul(sum_ps[:, j, :], counts[:, (b + g) % 2, j, :],
                                                    rows[:, b, part * D:(part + 1) * D],
                                                    start=part == 0, stop=part == PARTS - 1)
                    last.then_inc(s["summed"], 1)

                def row(r, b, nth, first):
                    for g in range(NG):
                        turn(r, g, first)
                        if g >= 2:
                            add_up(r * NG + g - 2, r, g - 2, b)
                        elif not first:
                            add_up(r * NG + g - 2, r - 1, NG + g - 2, 1 - b)
                        if g >= 1:
                            count(r * NG + g - 1, g - 1, b)
                        elif not first:
                            count(r * NG - 1, NG - 1, 1 - b)
                each_row(pe, NB, row)
                add_up(Q - 2, NB - 1, NG - 2, 0)
                count(Q - 1, NG - 1, 0)
                add_up(Q - 1, NB - 1, NG - 1, 0)

            @block.scalar
            def _(act):
                def take_counts(q, g, b):
                    act.wait_ge(s["counted"], q + 1)
                    nc.scalar.activation(counts[:, (b + g) % 2, :, :], cnt_ps[:, 0:G, :], ACT.Copy)\
                        .then_inc(s["counts_ready"], 1)

                def row(r, b, nth, first):
                    for g in range(NG):
                        act.wait_ge(s["src_turned"], r * NG + g + 1)
                        if not first:
                            act.wait_ge(stored[g], r * 16)
                        nc.scalar.activation(hot[:, g, 2, :].rearrange("p (j e) -> p j e", e=P), src_ps[:, 0:G, :],
                                             ACT.Copy, scale=float(HOT)).then_inc(s["hot_ready"], 1)
                        if g == 0:
                            nc.scalar.activation(rows[:, b, :],
                                                 k.table_s[:, bass.ds(r, 1), :, :].rearrange("p r a d -> p (r a d)"),
                                                 ACT.Copy).then_inc(s["rows_ready"], 1)
                        if g >= 1:
                            take_counts(r * NG + g - 1, g - 1, b)
                        elif not first:
                            take_counts(r * NG - 1, NG - 1, 1 - b)
                each_row(act, NB, row)
                take_counts(Q - 1, NG - 1, 0)

            @block.vector
            def _(dve):
                sums = nodes(k, k.one)
                dve.memset(k.one[:, :], 0.0).then_inc(s["added"], 1)
                dve.wait_ge(s["added"], 1)

                def take_dst(q, g, b):
                    dve.wait_ge(s["dst_turned"], q + 1)
                    dve.tensor_scalar(hot_d[:, (b + g) % 2, :, :], dst_ps[:, 0:G, :], float(HOT), None, ALU.mult)\
                        .then_inc(s["hot_d_ready"], 1)

                def add_in(q, g):
                    dve.wait_ge(s["summed"], q + 1)
                    dve.tensor_tensor(sums[:, g * G:(g + 1) * G, :], sums[:, g * G:(g + 1) * G, :], sum_ps[:, :, :],
                                      ALU.add).then_inc(s["added"], 1)

                def row(r, b, nth, first):
                    for g in range(NG):
                        dve.wait_ge(places_in[g], r * 16 + 16)
                        if not first:
                            dve.wait_ge(stored[g], r * 16)
                        for end in range(2):
                            last = dve.tensor_scalar(hot[:, g, end, :], places[:, g, :, end], k.pcol[:, 0:1], float(HOT),
                                                     ALU.is_equal, ALU.mult)
                        last.then_inc(s["hotT"], 1)
                        if g >= 1:
                            take_dst(r * NG + g - 1, g - 1, b)
                        elif not first:
                            take_dst(r * NG - 1, NG - 1, 1 - b)
                        if g >= 3:
                            add_in(r * NG + g - 3, g - 3)
                        elif not first:
                            add_in(r * NG + g - 3, NG + g - 3)
                each_row(dve, NB, row)
                take_dst(Q - 1, NG - 1, 0)
                for back in (3, 2, 1):
                    add_in(Q - back, NG - back)
                dve.wait_ge(s["added"], Q + 1)


def second_table(nc, k):
    with phase(nc, "value_ready root_ready step") as (s, block):
        block.scalar(sqrt_on_act(nc, k, s))

        @block.vector
        def _(dve):
            step = Chain(dve, s["step"])
            step(dve.tensor_tensor(k.res[:, :], k.res[:, :], k.one[:, :], ALU.add))
            normalise(k, s, step, nodes(k, k.res), nodes(k, k.cur), nodes(k, k.one))
            step(dve.tensor_tensor(k.res[:, :], k.res[:, :], k.cur[:, :], ALU.add))


def allocate_layers(nc, k, st):
    def sb(name, shape, dt):
        return st.enter_context(nc.sbuf_tensor(name, shape, dt))

    k.w1 = sb("w1", [k.D, 2 * k.D], F32)
    k.b1 = sb("b1", [2 * k.D, 1], F32)
    k.w2 = sb("w2", [2 * k.D, 2 * k.D], F32)
    k.b2 = sb("b2", [P, k.D], F32)
    k.w3 = sb("w3", [P, k.D], F32)
    k.b3 = sb("b3", [P, 1], F32)
    k.mask = sb("mask", [P, k.NB * k.NB], F32)
    k.sums = sb("sums", [P, k.NB], F32)


def node_products(nc, k, l, w):
    D, NB, BLK = k.D, k.NB, 4
    spans = [(a, min(a + BLK, NB)) for a in range(0, NB, BLK)]
    n = len(spans)
    with ExitStack() as st:
        def sb(name, shape, dt):
            return st.enter_context(nc.sbuf_tensor(name, shape, dt))

        def ps(name, shape, dt=F32):
            return st.enter_context(nc.psum_tensor(name, shape, dt))

        curT = sb("curT", [D, 2, BLK * P], F32)
        hid = sb("hid", [2 * D, 2, BLK * P], F32)
        rest = sb("rest", [P, NB * D], F32)
        turn_ps = [ps(f"turn_ps{i}", [D, BLK * P]) for i in range(2)]
        hid_ps = [ps(f"hid_ps{i}", [2 * D, BLK * P]) for i in range(2)]
        att_ps = [ps(f"att_ps{i}", [P, BLK, 2 * D]) for i in range(2)]
        with phase(nc, "cleared weights turned curT_ready hidden hid_ready attended taken step", again=True) as (s, block):
            @block.sync
            def _(sp):
                def col(a):
                    return a[bass.ds(l, 1), :].rearrange("o d -> d o")

                at = bass.ds(l, 1)
                loads = [
                    (k.w1[:, 0:D], w.nb_w[at, :, :].rearrange("o a b -> (o a) b")),
                    (k.w1[:, D:2 * D], w.self_w[at, :, :].rearrange("o a b -> (o a) b")),
                    (k.b1[0:D, :], col(w.nb_b)), (k.b1[D:2 * D, :], col(w.self_b)),
                    (k.b2[:, :], w.att1_b[at, :].rearrange("o d -> (o d)").partition_broadcast(P)),
                    (k.w3[:, :], w.att2_w[at, :, :].rearrange("o d x -> (o d x)").partition_broadcast(P)),
                    (k.b3[:, :], w.att2_b[at, :].rearrange("o x -> (o x)").partition_broadcast(P)),
                ]
                for dst, src in loads:
                    sp.dma_start(dst, src).then_inc(s["weights"], 16)
                sp.wait_ge(s["cleared"], 1)
                for h in range(2):
                    sp.dma_start(k.w2[h * D:(h + 1) * D, h * D:(h + 1) * D],
                                 w.att1_w[at, h * D:(h + 1) * D, :].rearrange("o a b -> (o a) b"))\
                        .then_inc(s["weights"], 16)

            @block.tensor
            def _(pe):
                cur = nodes(k, k.cur)

                def turn(m):
                    a, z = spans[m]
                    if m >= 2:
                        pe.wait_ge(s["curT_ready"], m - 1)
                    for blk in range(a, z):
                        last = nc.tensor.transpose(turn_ps[m % 2][:, (blk - a) * P:(blk - a + 1) * P],
                                                   cur[:, blk, :], k.ident[:, :])
                    last.then_inc(s["turned"], 1)

                def hide(m):
                    a, z = spans[m]
                    pe.wait_ge(s["curT_ready"], m + 1)
                    if m >= 2:
                        pe.wait_ge(s["hid_ready"], m - 1)
                    nc.tensor.matmul(hid_ps[m % 2][:, 0:(z - a) * P], k.w1[:, :], curT[:, m % 2, 0:(z - a) * P],
                                     start=True, stop=True).then_inc(s["hidden"], 1)

                def attend(m):
                    a, z = spans[m]
                    pe.wait_ge(s["hid_ready"], m + 1)
                    if m >= 2:
                        pe.wait_ge(s["taken"], m - 1)
                    for j in range(z - a):
                        last = nc.tensor.matmul(att_ps[m % 2][:, j, :], hid[:, m % 2, j * P:(j + 1) * P], k.w2[:, :],
                                                start=True, stop=True)
                    last.then_inc(s["attended"], 1)

                pe.wait_ge(s["weights"], 16 * 9)
                for m in range(n + 2):
                    if m < n:
                        turn(m)
                    if 0 <= m - 1 < n:
                        hide(m - 1)
                    if m >= 2:
                        attend(m - 2)

            @block.scalar
            def _(act):
                act.wait_ge(s["weights"], 16 * 9)

                def relu(m):
                    a, z = spans[m]
                    act.wait_ge(s["hidden"], m + 1)
                    if m >= 2:
                        act.wait_ge(s["attended"], m - 1)
                    nc.scalar.activation(hid[:, m % 2, 0:(z - a) * P], hid_ps[m % 2][:, 0:(z - a) * P], ACT.Relu,
                                         bias=k.b1[:, 0:1]).then_inc(s["hid_ready"], 1)

                for m in range(n + 1):
                    if m < n:
                        a, z = spans[m]
                        act.wait_ge(s["turned"], m + 1)
                        if m >= 2:
                            act.wait_ge(s["hidden"], m - 1)
                        nc.scalar.activation(curT[:, m % 2, 0:(z - a) * P], turn_ps[m % 2][:, 0:(z - a) * P],
                                             ACT.Copy).then_inc(s["curT_ready"], 1)
                    if m >= 1:
                        relu(m - 1)

            @block.vector
            def _(dve):
                step = Chain(dve, s["step"])
                dve.memset(k.w2[:, :], 0.0).then_inc(s["cleared"], 1)
                dve.wait_ge(s["weights"], 16 * 9)
                for m, (a, z) in enumerate(spans):
                    dve.wait_ge(s["attended"], m + 1)
                    dve.tensor_copy(nodes(k, k.one)[:, a:z, :], att_ps[m % 2][:, 0:z - a, 0:D])
                    dve.tensor_tensor(nodes(k, k.two)[:, a:z, :], att_ps[m % 2][:, 0:z - a, D:2 * D],
                                      k.b2[:, :].unsqueeze(1).to_broadcast([P, z - a, D]), ALU.add).then_inc(s["taken"], 1)
                dve.wait_ge(s["taken"], n)
                split3(k, step, k.table_s, nodes(k, k.one), nodes(k, rest))
                split3(k, step, k.table_d, nodes(k, k.two), nodes(k, rest))


def edge_masks(nc, k):
    NB, G, NG, D = k.NB, k.G, k.NG, k.D
    MID = NG // 2
    with ExitStack() as st:
        def sb(name, shape, dt):
            return st.enter_context(nc.sbuf_tensor(name, shape, dt))

        def ps(name, shape, dt=F32):
            return st.enter_context(nc.psum_tensor(name, shape, dt))

        hot = sb("hot_a", [P, 2, NG, 3, G * P], U8)
        rows = sb("rows_a", [P, 2, PARTS * D], BF16)
        weighed = sb("weighed", [P, 2, G, D], F32)
        logit = sb("logit", [P, 2, NB], F32)
        gate = sb("gate", [P, 2, NB], F32)
        fresh = sb("fresh", [P, NB], F32)
        parts = sb("parts", [P, NB, PARTS], BF16)
        pre_ps = [ps(f"pre_ps{i}", [P, 8, D]) for i in range(4)]
        total_ps = [ps(f"total_ps{i}", [P, PARTS + 1]) for i in range(2)]
        sems = " ".join([f"in{b}_{g}" for b in range(2) for g in range(NG)])
        with phase(nc, "passed rows_ready gathered weigh logits gated parts_ready summed taken step pool_step "
                       + sems, again=True) as (s, block):
            loaded = [[s[f"in{b}_{g}"] for g in range(NG)] for b in range(2)]

            @block.sync
            def _(sp):
                def row(r, b, nth, first):
                    for g in range(NG):
                        wait_count(sp, s, s["summed"], r + 1)
                        sp.dma_start(hot[:, b, g, :, :],
                                     k.hot_dram[bass.ds(r, 1), :, g, :, :].rearrange("r p a b -> (r p) a b"))\
                            .then_inc(loaded[b][g], 16)
                each_row(sp, NB, row)

            @block.tensor
            def _(pe):
                pe.sem_inc(s["summed"], 2)
                pe.sem_inc(s["gathered"], NG)

                def gather(q, r, g, b, nth):
                    pe.wait_ge(loaded[b][g], nth * 16)
                    pe.wait_ge(s["weigh"], q + 1)
                    if g == 0:
                        pe.wait_ge(s["rows_ready"], r + 1)
                    carry_waits(nc, k, pre_ps[g % 4][:, 7, 0:1])
                    for j in range(G):
                        d = (g * G + j)
                        for end in range(2):
                            for part in range(PARTS):
                                table = rows[:, b, part * D:(part + 1) * D] if end == 0 else k.table_d[:, d, part, :]
                                last = nc.tensor.matmul(pre_ps[g % 4][:, j, :], hot[:, b, g, end, j * P:(j + 1) * P].bitcast(FP8),
                                                        table, start=end + part == 0, stop=end == 1 and part == 2)
                    last.then_inc(s["gathered"], 1)

                def sum_masks(r, b):
                    pe.wait_ge(s["parts_ready"], r + 1)
                    pe.wait_ge(s["taken"], r + 1)
                    carry_waits(nc, k, total_ps[b][:, PARTS:PARTS + 1])
                    for g in range(NG):
                        for j in range(G):
                            t = g * G + j
                            last = nc.tensor.matmul(total_ps[b][:, 0:PARTS], hot[:, b, g, 2, j * P:(j + 1) * P].bitcast(FP8),
                                                    parts[:, t, :], start=t == 0, stop=t == NB - 1)
                    last.then_inc(s["summed"], 1)

                def row(r, b, nth, first):
                    for g in range(NG):
                        gather(r * NG + g, r, g, b, nth)
                        if g == MID and not first:
                            sum_masks(r - 1, 1 - b)
                each_row(pe, NB, row)
                sum_masks(NB - 1, 0)

            @block.scalar
            def _(act):
                def gates(r, b):
                    act.wait_ge(s["logits"], r * NG + NG)
                    nc.scalar.activation(gate[:, b, :], logit[:, b, :], ACT.Sigmoid, bias=k.b3[:, 0:1])\
                        .then_inc(s["gated"], 1)

                def row(r, b, nth, first):
                    if not first:
                        act.wait_ge(s["gathered"], r * NG)
                    nc.scalar.activation(rows[:, b, :],
                                         k.table_s[:, bass.ds(r, 1), :, :].rearrange("p r a d -> p (r a d)"),
                                         ACT.Copy).then_inc(s["rows_ready"], 1)
                    if not first:
                        gates(r - 1, 1 - b)
                each_row(act, NB, row)
                gates(NB - 1, 0)

            @block.gpsimd
            def _(pool):
                def row(r, b, nth, first):
                    pool.sem_clear(s["pool_step"])
                    step = Chain(pool, s["pool_step"])
                    wait_count(pool, s, s["gated"], r + 1)
                    step(pool.tensor_scalar(fresh[:, :], gate[:, b, :], ZETA - GAMMA, GAMMA, ALU.mult, ALU.add))
                    step(pool.tensor_scalar(fresh[:, :], fresh[:, :], 0.0, 1.0, ALU.max, ALU.min))
                    pool.tensor_copy(k.mask[:, bass.ds(r * NB, NB)], fresh[:, :])
                    step(pool.tensor_copy(parts[:, :, 0], fresh[:, :]))
                    step(pool.tensor_tensor(fresh[:, :], fresh[:, :], parts[:, :, 0], ALU.subtract))
                    step(pool.tensor_copy(parts[:, :, 1], fresh[:, :]))
                    step(pool.tensor_tensor(fresh[:, :], fresh[:, :], parts[:, :, 1], ALU.subtract))
                    step(pool.tensor_copy(parts[:, :, 2], fresh[:, :]))
                    pool.sem_inc(s["parts_ready"], 1)
                each_row(pool, NB, row)

            @block.vector
            def _(dve):
                dve.sem_inc(s["weigh"], 3)
                dve.sem_inc(s["taken"], 2)

                def reduce(q, g, b):
                    dve.wait_ge(s["weigh"], q + 4)
                    dve.tensor_reduce(logit[:, b, g * G:(g + 1) * G], weighed[:, (b + g) % 2, :, :], X, ALU.add)\
                        .then_inc(s["logits"], 1)

                def take(r, b):
                    dve.wait_ge(s["summed"], r + 3)
                    dve.tensor_reduce(k.sums[:, bass.ds(r, 1)], total_ps[b][:, 0:PARTS], X, ALU.add).then_inc(s["taken"], 1)

                def row(r, b, nth, first):
                    for g in range(NG):
                        q = r * NG + g
                        if not (first and g < 2):
                            dve.wait_ge(s["logits"], q - 1)
                        dve.wait_ge(s["gathered"], q + NG + 1)
                        dve.scalar_tensor_tensor(weighed[:, (b + g) % 2, :, :], pre_ps[g % 4][:, 0:G, :], 0.0,
                                                 k.w3[:, :].unsqueeze(1).to_broadcast([P, G, D]),
                                                 ALU.max, ALU.mult).then_inc(s["weigh"], 1)
                        if g >= 1:
                            reduce(q - 1, g - 1, b)
                        elif not first:
                            reduce(q - 1, NG - 1, 1 - b)
                    if not first:
                        take(r - 1, 1 - b)
                each_row(dve, NB, row)
                reduce(NB * NG - 1, NG - 1, 0)
                take(NB - 1, 0)
                dve.wait_ge(s["taken"], NB + 2)


def scale_rows(nc, k):
    with phase(nc, "value_ready root_ready step", again=True) as (s, block):
        block.scalar(sqrt_on_act(nc, k, s))

        @block.vector
        def _(dve):
            step = Chain(dve, s["step"])
            dve.tensor_scalar(k.var[:, :], k.sums[:, :], EPS_SUM, None, ALU.add).then_inc(s["value_ready"], 1)
            inverse_root(s, step, k.var[:, :], k.root[:, :], k.inv[:, :], k.mean[:, :])
            step(dve.tensor_scalar(k.inv[:, :], k.inv[:, :], 0.0, D_MAX, ALU.max, ALU.min))
            step(dve.tensor_tensor(nodes(k, k.one), nodes(k, k.cur),
                                   k.inv[:, :].unsqueeze(2).to_broadcast([P, k.NB, k.D]), ALU.mult))
            split3(k, step, k.table_d, nodes(k, k.one), nodes(k, k.two))


def sum_messages(nc, k):
    NB, G, NG, D = k.NB, k.G, k.NG, k.D
    Q = NB * NG
    with ExitStack() as st:
        def sb(name, shape, dt):
            return st.enter_context(nc.sbuf_tensor(name, shape, dt))

        def ps(name, shape, dt=F32):
            return st.enter_context(nc.psum_tensor(name, shape, dt))

        hot = sb("hot_b", [P, NG, 2, G * P], U8)
        hot_f = sb("hot_f", [P, 2, G, P], F32)
        message = sb("message", [P, 2, G, D], F32)
        row_ps = [ps(f"row_ps{i}", [P, 8, D]) for i in range(4)]
        sum_ps = [ps(f"sum_ps{i}", [P, D]) for i in range(2)]
        sems = " ".join([f"in{g}" for g in range(NG)])
        with phase(nc, "passed gathered scaled widened added summed taken " + sems, again=True) as (s, block):
            loaded = [s[f"in{g}"] for g in range(NG)]

            @block.sync
            def _(sp):
                def row(r, b, nth, first):
                    for g in range(NG):
                        if not first:
                            wait_count(sp, s, s["gathered"], (r - 1) * NG + g + 1)
                            wait_count(sp, s, s["widened"], (r - 1) * NG + g + 1)
                        sp.dma_start(hot[:, g, :, :],
                                     k.hot_dram[bass.ds(r, 1), :, g, 1:3, :].rearrange("r p a b -> (r p) a b"))\
                            .then_inc(loaded[g], 16)
                each_row(sp, NB, row)

            @block.tensor
            def _(pe):
                def gather(q, r, g):
                    pe.wait_ge(loaded[g], r * 16 + 16)
                    pe.wait_ge(s["scaled"], q + 1)
                    carry_waits(nc, k, row_ps[g % 4][:, 7, 0:1])
                    for j in range(G):
                        for part in range(PARTS):
                            last = nc.tensor.matmul(row_ps[g % 4][:, j, :], hot[:, g, 0, j * P:(j + 1) * P].bitcast(FP8),
                                                    k.table_d[:, g * G + j, part, :],
                                                    start=part == 0, stop=part == PARTS - 1)
                    last.then_inc(s["gathered"], 1)

                def add_up(q, r, g, b):
                    pe.wait_ge(s["scaled"], q + 4)
                    pe.wait_ge(s["widened"], q + 1)
                    if g == 0:
                        pe.wait_ge(s["taken"], r + 1)
                    for j in range(G):
                        t = g * G + j
                        last = nc.tensor.matmul(sum_ps[b][:, :], hot_f[:, (b + g) % 2, j, :],
                                                message[:, (b + g) % 2, j, :], start=t == 0, stop=t == NB - 1)
                    last.then_inc(s["added"], 1)

                def row(r, b, nth, first):
                    for g in range(NG):
                        gather(r * NG + g, r, g)
                        if g >= 2:
                            add_up(r * NG + g - 2, r, g - 2, b)
                        elif not first:
                            add_up(r * NG + g - 2, r - 1, NG + g - 2, 1 - b)
                each_row(pe, NB, row)
                add_up(Q - 2, NB - 1, NG - 2, 0)
                add_up(Q - 1, NB - 1, NG - 1, 0)

            @block.scalar
            def _(act):
                act.sem_inc(s["taken"], 2)

                def take(r, b):
                    act.wait_ge(s["added"], r * NG + NG)
                    nc.scalar.activation(k.cur[:, bass.ds(r * D, D)], sum_ps[b][:, :], ACT.Copy).then_inc(s["taken"], 1)

                def row(r, b, nth, first):
                    for g in range(NG):
                        act.wait_ge(loaded[g], r * 16 + 16)
                        if not (first and g < 2):
                            act.wait_ge(s["added"], r * NG + g - 1)
                        nc.scalar.activation(hot_f[:, (b + g) % 2, :, :],
                                             hot[:, g, 1, :].rearrange("p (j e) -> p j e", e=P), ACT.Copy, scale=1.0 / HOT)\
                            .then_inc(s["widened"], 1)
                        if g == 2 and not first:
                            take(r - 1, 1 - b)
                each_row(act, NB, row)
                take(NB - 1, 0)
                act.wait_ge(s["taken"], NB + 2)

            @block.vector
            def _(dve):
                dve.sem_inc(s["scaled"], 3)

                def row(r, b, nth, first):
                    for g in range(NG):
                        q = r * NG + g
                        dve.wait_ge(s["gathered"], q + 1)
                        if not (first and g < 2):
                            dve.wait_ge(s["added"], q - 1)
                        dve.tensor_tensor(message[:, (b + g) % 2, :, :], row_ps[g % 4][:, 0:G, :],
                                          k.mask[:, bass.ds(r * NB + g * G, G)].unsqueeze(2).to_broadcast([P, G, D]),
                                          ALU.mult).then_inc(s["scaled"], 1)
                each_row(dve, NB, row)


def end_layer(nc, k):
    with phase(nc, "step", again=True) as (s, block):
        @block.vector
        def _(dve):
            step = Chain(dve, s["step"])
            step(dve.tensor_tensor(nodes(k, k.cur), nodes(k, k.cur),
                                   k.inv[:, :].unsqueeze(2).to_broadcast([P, k.NB, k.D]), ALU.mult))
            step(dve.tensor_tensor(k.res[:, :], k.res[:, :], k.cur[:, :], ALU.add))


def store(nc, k, out):
    whole = k.N // P
    with phase(nc, "stored") as (s, block):
        @block.sync
        def _(sp):
            sp.dma_start(out[0:whole * P, :].rearrange("(b p) d -> p b d", p=P),
                         nodes(k, k.res)[:, 0:whole, :]).then_inc(s["stored"], 16)
            if k.N > whole * P:
                sp.dma_start(out[whole * P:k.N, :], nodes(k, k.res)[0:k.N - whole * P, whole, :]).then_inc(s["stored"], 16)
            sp.wait_ge(s["stored"], 16 * (1 + (k.N > whole * P)))


def gnn(nc, x, src, dst, nb_w, nb_b, self_w, self_b, att1_w, att1_b, att2_w, att2_b, out, cap=P):
    k = make_plan(x, src, dst, nb_w, out, cap)
    w = Record()
    w.nb_w, w.nb_b, w.self_w, w.self_b = nb_w, nb_b, self_w, self_b
    w.att1_w, w.att1_b, w.att2_w, w.att2_b = att1_w, att1_b, att2_w, att2_b
    k.slots_dram = nc.dram_tensor("slots_scratch", [k.SLOTS, 2], BF16).ap()
    k.hot_dram = nc.dram_tensor("hot_scratch", [k.NB, P, k.NG, 3, k.G * P], U8).ap()
    k.rows_a_dram = nc.dram_tensor("rows_a_scratch", [k.NB * P, k.D], F32).ap()
    k.rows_b_dram = nc.dram_tensor("rows_b_scratch", [k.NB * P, k.D], F32).ap()
    with ExitStack() as st:
        allocate(nc, k, st)
        with ExitStack() as sort_st:
            allocate_sort(nc, k, sort_st)
            constants(nc, k)
            load_edges(nc, k, src, dst)
            sort_edges(nc, k)
        count_spills(nc, k)
        first_table(nc, k, x)
        build_and_sum(nc, k)
        spilled_edges(nc, k, [(k.cur, k.rows_a_dram)], [(k.rows_a_dram, k.srci)], k.dsti, nodes(k, k.one), k.D, "hop")
        second_table(nc, k)
        allocate_layers(nc, k, st)
        with nc.Fori(0, k.L) as l:
            node_products(nc, k, l, w)
            edge_masks(nc, k)
            spilled_edges(nc, k, [(k.one, k.rows_a_dram), (k.two, k.rows_b_dram)],
                          [(k.rows_a_dram, k.srci), (k.rows_b_dram, k.dsti)], k.srci,
                          k.sums[:, :].unsqueeze(2), 1, "masks")
            scale_rows(nc, k)
            sum_messages(nc, k)
            spilled_edges(nc, k, [(k.one, k.rows_a_dram)], [(k.rows_a_dram, k.dsti)], k.srci, nodes(k, k.cur), k.D, "messages")
            end_layer(nc, k)
        store(nc, k, out)


_INS = ["x", "src", "dst", "L1_gnn_nb_W", "L1_gnn_nb_b", "L1_gnn_self_W", "L1_gnn_self_b",
        "L1_gnn_att1_W", "L1_gnn_att1_b", "L1_gnn_att2_W", "L1_gnn_att2_b"]


def kernel(**inputs):
    import numpy as _np
    import concourse.bacc as _bacc
    from concourse import mybir as _mybir
    from concourse.bass_utils import run_bass_kernel_spmd as _run

    nc = _bacc.Bacc("TRN2", target_bir_lowering=False, num_devices=1)
    arrays, args = {}, []
    for name in _INS:
        a = _np.ascontiguousarray(inputs[name])
        arrays[f"in_{name}"] = a
        args.append(nc.dram_tensor(f"in_{name}", a.shape, _mybir.dt.from_np(a.dtype), kind="ExternalInput").ap())
    shape = inputs["x"].shape
    args.append(nc.dram_tensor("out_0", shape, _mybir.dt.float32, kind="ExternalOutput").ap())
    gnn(nc, *args)
    r = _run(nc, [arrays], core_ids=[0])
    return r.results[0]["out_0"]
```

```python
import concourse.bass as bass
from concourse import mybir
from contextlib import ExitStack, contextmanager

F32 = mybir.dt.float32
F16 = mybir.dt.float16
BF16 = mybir.dt.bfloat16
FP8 = mybir.dt.float8e4
I32 = mybir.dt.int32
U8 = mybir.dt.uint8
ALU = mybir.AluOpType
ACT = mybir.ActivationFunctionType
X = mybir.AxisListType.X

P = 128
PARTS = 3
CH = 8
HOT = 56
EMPTY = 255
GAMMA, ZETA = -0.45, 1.05
EPS_LN, EPS_SUM, D_MAX = 1e-5, 1e-6, 10.0



class Record:
    pass


class Chain:

    def __init__(self, eng, sem, base=0):
        self.eng, self.sem, self.base, self.n = eng, sem, base, 0

    def __call__(self, ins):
        ins.then_inc(self.sem, 1)
        self.n += 1
        self.eng.wait_ge(self.sem, self.base + self.n)


def hold_waits(eng, s):
    eng.sem_inc(s["passed"], 1)


def wait_count(eng, s, sem, value):
    eng.wait_ge(sem, value)
    if not isinstance(value, int):
        hold_waits(eng, s)


@contextmanager
def phase(nc, names, again=False):
    with ExitStack() as st:
        sems = {n: st.enter_context(nc.semaphore(n)) for n in names.split()}
        with nc.Block() as block:
            yield sems, block
        if again:
            zero(nc, sems)


def zero(nc, sems):
    numbers = [h.num for h in sems.values()]
    assert max(numbers) - min(numbers) + 1 == len(numbers)
    nc.gpsimd.sem_clear(range(min(numbers), max(numbers) + 1))


@contextmanager
def spill_phase(nc, k):
    with nc.Block() as block:
        yield k.spill_sems, block
    numbers = [h.num for h in k.spill_sems.values()]
    nc.gpsimd.dma_reset(range(min(numbers), max(numbers) + 1))
    zero(nc, k.spill_sems)
    nc.all_engine_barrier()


def each_row(eng, nb, row):
    row(0, 0, 1, True)
    with eng.Fori(0, (nb - 1) // 2) as i:
        row(i * 2 + 1, 1, i + 1, False)
        row(i * 2 + 2, 0, i + 2, False)


def make_plan(x, src, dst, nb_w, out, cap):
    k = Record()
    k.N, k.D = x.shape
    k.E = src.shape[0]
    k.L = nb_w.shape[0]
    k.NB = -(-k.N // P)
    assert k.NB % 2 == 1 and k.D == 64
    k.G = max(g for g in range(1, 8) if k.NB % g == 0)
    k.NG = k.NB // k.G
    k.NT = -(-k.E // (P * 2 * CH)) * 2 * CH
    k.NTP = k.NT + CH
    k.SLOTS = k.NB * k.NB * P
    k.PAD = k.NB * P
    k.MID = k.NB * k.NB // 2
    assert k.NB * k.NB + k.NB - k.MID < 2048
    k.CAP = cap
    return k


def allocate(nc, k, st):
    def sb(name, shape, dt):
        return st.enter_context(nc.sbuf_tensor(name, shape, dt))

    k.iota = sb("iota", [P, P], F32)
    k.pcol = sb("pcol", [P, 1], F32)
    k.ident = sb("ident", [P, P], F32)
    k.ident16 = sb("ident16", [P, P], F16)
    k.identb = sb("identb", [P, P], BF16)
    k.before = sb("before", [P, P], BF16)
    k.ones = sb("ones", [P, P], F32)
    k.zero = sb("zero", [P, P], BF16)
    k.srci = sb("srci", [P, k.NTP], I32)
    k.dsti = sb("dsti", [P, k.NTP], I32)
    k.spill = sb("spill", [P, k.NT], F32)
    k.res = sb("res", [P, k.NB * k.D], F32)
    k.cur = sb("cur", [P, k.NB * k.D], F32)
    k.both = sb("both", [P, k.NB, 2 * k.D], F32)
    k.one, k.two = k.both[:, :, 0:k.D], k.both[:, :, k.D:2 * k.D]
    k.table = sb("table", [P, k.NB, PARTS, 2 * k.D], BF16)
    k.table_s, k.table_d = k.table[:, :, :, 0:k.D], k.table[:, :, :, k.D:2 * k.D]
    k.mean = sb("mean", [P, k.NB], F32)
    k.var = sb("var", [P, k.NB], F32)
    k.root = sb("root", [P, k.NB], F32)
    k.inv = sb("inv", [P, k.NB], F32)
    k.col_spills = sb("col_spills", [1, k.NT], I32)
    k.some_spill = sb("some_spill", [1, 1], I32)
    k.spill_mask = sb("spill_mask", [P, k.NT], F32)
    names = "spill_stored picked gathered_rows placed multiplied step"
    k.spill_sems = {n: st.enter_context(nc.semaphore("spill_" + n)) for n in names.split()}


def allocate_sort(nc, k, st):
    def sb(name, shape, dt):
        return st.enter_context(nc.sbuf_tensor(name, shape, dt))

    k.itmp = sb("itmp", [P, k.NTP], I32)
    k.bs = sb("bs", [P, k.NTP], F32)
    k.bd = sb("bd", [P, k.NTP], F32)
    k.place = sb("place", [P, k.NTP, 2], U8)
    k.key = sb("key", [P, k.NTP], F32)
    k.key16 = sb("key16", [P, k.NTP], F16)
    k.empty = sb("empty", [P, -(-k.SLOTS // (2 * P)) * 2 + 2], U8)


def constants(nc, k):
    with phase(nc, "iota_done made") as (s, block):
        @block.gpsimd
        def _(pool):
            nc.gpsimd.iota(k.iota[:, :], [[1, P]], base=0, channel_multiplier=0,
                           allow_small_or_imprecise_dtypes=True).then_inc(s["iota_done"], 1)
            nc.gpsimd.iota(k.pcol[:, :], [[0, 1]], base=0, channel_multiplier=1,
                           allow_small_or_imprecise_dtypes=True).then_inc(s["iota_done"], 1)

        @block.vector
        def _(dve):
            dve.wait_ge(s["iota_done"], 2)
            for t in (k.ident, k.ident16, k.identb):
                nc.vector.tensor_scalar(t[:, :], k.iota[:, :], k.pcol[:, 0:1], None, ALU.is_equal)
            nc.vector.tensor_scalar(k.before[:, :], k.iota[:, :], k.pcol[:, 0:1], None, ALU.is_lt)
            nc.vector.memset(k.ones[:, :], 1.0)
            nc.vector.memset(k.zero[:, :], 0.0).then_inc(s["made"], 1)
            dve.wait_ge(s["made"], 1)


def load_inputs(nc, k, src, dst, x):
    whole = k.N // P
    full, rest = k.E // k.NT, k.E % k.NT
    cuts = [c for c in (0, full // 16 * 16, full) if c <= full]
    spans = [(a, b) for a, b in zip(cuts, cuts[1:]) if b > a]
    n_loads = 2 * (len(spans) + (rest > 0))
    with phase(nc, "padded loaded rows_padded rows_loaded step") as (s, block):
        @block.sync
        def _(sp):
            sp.wait_ge(s["padded"], 2)
            for e, t in ((src, k.srci), (dst, k.dsti)):
                for a, b in spans:
                    sp.dma_start(t[a:b, 0:k.NT],
                                 e[a * k.NT:b * k.NT].rearrange("(p t) -> p t", t=k.NT)).then_inc(s["loaded"], 16)
                if rest:
                    sp.dma_start(t[full:full + 1, 0:rest],
                                 e[full * k.NT:k.E].rearrange("(p t) -> p t", p=1)).then_inc(s["loaded"], 16)
            sp.wait_ge(s["rows_padded"], 1)
            sp.dma_start(nodes(k, k.res)[:, 0:whole, :],
                         x[0:whole * P, :].rearrange("(b p) d -> p b d", p=P)).then_inc(s["rows_loaded"], 16)
            if k.N > whole * P:
                sp.dma_start(nodes(k, k.res)[0:k.N - whole * P, whole, :], x[whole * P:k.N, :])\
                    .then_inc(s["rows_loaded"], 16)
            sp.wait_ge(s["rows_loaded"], 16 * (1 + (k.N > whole * P)))

        @block.vector
        def _(dve):
            step = Chain(dve, s["step"])
            nc.vector.memset(k.srci[:, :], k.PAD).then_inc(s["padded"], 1)
            nc.vector.memset(k.dsti[:, :], k.PAD).then_inc(s["padded"], 1)
            nc.vector.memset(k.res[:, :], 0.0).then_inc(s["rows_padded"], 1)
            dve.wait_ge(s["padded"], 2)
            dve.wait_ge(s["loaded"], 16 * n_loads)
            for n, (ends, blk) in enumerate(((k.srci, k.bs), (k.dsti, k.bd))):
                step(nc.vector.tensor_single_scalar(k.itmp[:, :], ends[:, :], 7, ALU.logical_shift_right))
                step(nc.vector.tensor_copy(blk[:, :], k.itmp[:, :]))
                step(nc.vector.tensor_single_scalar(k.itmp[:, :], ends[:, :], P - 1, ALU.bitwise_and))
                step(nc.vector.tensor_copy(k.place[:, :, n], k.itmp[:, :]))
            step(nc.vector.scalar_tensor_tensor(k.key[:, :], k.bs[:, :], float(k.NB), k.bd[:, :], ALU.mult, ALU.add))
            step(nc.vector.tensor_scalar(k.key16[:, :], k.key[:, :], float(-k.MID), None, ALU.add))
            step(nc.vector.memset(k.empty[:, :], EMPTY))


def sort_edges(nc, k):
    NB, NPAIR = k.NB, k.NT // (2 * CH)
    with ExitStack() as st:
        def sb(name, shape, dt):
            return st.enter_context(nc.sbuf_tensor(name, shape, dt))

        def ps(name, shape, dt=F32):
            return st.enter_context(nc.psum_tensor(name, shape, dt))

        key_st = sb("key_st", [P, 2, CH], F16)
        one_s = sb("one_s", [P, 2, CH, NB], BF16)
        one_d = sb("one_d", [P, 2, CH, NB], BF16)
        one_sT = sb("one_sT", [NB, CH, P], F32)
        count_sb = sb("count_sb", [NB, 2, NB], F32)
        same = sb("same", [P, CH, P], BF16)
        picked = sb("picked", [P, CH, NB], F32)
        before_col = sb("before_col", [P, CH], F32)
        in_col = sb("in_col", [P, 2, CH], F32)
        rank = sb("rank", [P, CH], F32)
        over = sb("over", [P, CH], F32)
        slot_f = sb("slot_f", [P, CH], F32)
        slot = sb("slot", [P, 2, CH], I32)
        place_st = sb("place_st", [P, 2, CH, 2], U8)
        rows_ps = [ps(f"rows_ps{i}", [P, CH, P]) for i in range(2)]
        one_sT_ps = ps("one_sT_ps", [NB, CH, P], BF16)
        before_ps = [ps(f"before_ps{i}", [P, CH, NB]) for i in range(2)]
        count_ps = ps("count_ps", [NB, NB])

        with phase(nc, "passed init_a init_b staged rows transposed one_sT_ready counted count_ready ranked slots_ready "
                       "value_ready root_ready step") as (s, block):
            scattered = [s["init_a"], s["init_b"]]

            @block.gpsimd
            def _(pool):
                for h in range(2):
                    lo, hi = (0, k.NB * k.NB // 2 * P) if h == 0 else (k.NB * k.NB // 2 * P, k.SLOTS)
                    pool.dma_start(k.slots_dram[lo:hi, :].rearrange("(p a) b -> p (a b)", p=P),
                                   k.empty[:, 0:(hi - lo) // P * 2]).then_inc(scattered[h], 16)
                for h in range(2):
                    pool.wait_ge(scattered[h], 16)
                with pool.Fori(0, NPAIR) as i:
                    for b in range(2):
                        wait_count(pool, s, s["slots_ready"], i * 2 + b + 1)
                        for j in range(CH):
                            nc.gpsimd.indirect_dma_start(
                                out=k.slots_dram[:, :],
                                out_offset=bass.IndirectOffsetOnAxis(ap=slot[:, b, j:j + 1], axis=0),
                                in_=place_st[:, b, j, :], in_offset=None,
                                bounds_check=k.SLOTS - 1, oob_is_err=False).then_inc(scattered[b], 16)
                for h in range(2):
                    pool.wait_ge(scattered[h], 16 + 16 * CH * NPAIR)

            @block.tensor
            def _(pe):
                nc.tensor.matmul(count_ps[:, :], k.zero[:, 0:NB], k.zero[:, 0:NB], start=True, stop=False,
                                 skip_group_check=True).then_inc(s["counted"], 1)
                with pe.Fori(0, NPAIR) as i:
                    for b in range(2):
                        chunk = i * 2 + b
                        pe.wait_ge(s["staged"], chunk + 1)
                        for j in range(CH):
                            last = nc.tensor.matmul(rows_ps[b][:, j, :], key_st[:, b, j:j + 1].to_broadcast([P, P]),
                                                    k.ident16[:, :], start=True, stop=True)
                        last.then_inc(s["rows"], 1)
                        for j in range(CH):
                            last = nc.tensor.transpose(one_sT_ps[:, j, :], one_s[:, b, j, :], k.identb[:, :])
                        last.then_inc(s["transposed"], 1)
                        pe.wait_ge(s["one_sT_ready"], chunk + 1)
                        for j in range(CH):
                            t = i * (2 * CH) + b * CH + j
                            pe.wait_ge(s["count_ready"], t + 1)
                            nc.tensor.matmul(count_ps[:, :], one_s[:, b, j, :], one_d[:, b, j, :],
                                             start=False, stop=False, skip_group_check=True).then_inc(s["counted"], 1)
                            last = nc.tensor.matmul(before_ps[b][:, j, :], one_sT[:, j, :],
                                                    count_sb[:, j % 2, :], start=True, stop=True)
                        last.then_inc(s["ranked"], 1)

            @block.scalar
            def _(act):
                act.wait_ge(s["counted"], 1)
                nc.scalar.activation(count_sb[:, 0, :], count_ps[:, :], ACT.Copy).then_inc(s["count_ready"], 1)
                with act.Fori(0, NPAIR) as i:
                    for b in range(2):
                        act.wait_ge(s["transposed"], i * 2 + b + 1)
                        nc.scalar.activation(one_sT[:, :, :], one_sT_ps[:, :, :], ACT.Copy).then_inc(s["one_sT_ready"], 1)
                        for j in range(CH):
                            act.wait_ge(s["counted"], i * (2 * CH) + b * CH + j + 2)
                            nc.scalar.activation(count_sb[:, (j + 1) % 2, :], count_ps[:, :],
                                                 ACT.Copy).then_inc(s["count_ready"], 1)
                sqrt_on_act(nc, k, s)(act)

            @block.vector
            def _(dve):
                def stage(chunk, b):
                    at = bass.ds(chunk * CH, CH)
                    nc.vector.tensor_copy(key_st[:, b, :], k.key16[:, at])
                    for one, blk in ((one_s, k.bs), (one_d, k.bd)):
                        last = nc.vector.tensor_tensor(
                            one[:, b, :, :], k.iota[:, 0:NB].unsqueeze(1).to_broadcast([P, CH, NB]),
                            blk[:, at].unsqueeze(2).to_broadcast([P, CH, NB]), ALU.is_equal)
                    last.then_inc(s["staged"], 1)

                stage(0, 0)
                with dve.Fori(0, NPAIR) as i:
                    for b in range(2):
                        chunk = i * 2 + b
                        at = bass.ds(chunk * CH, CH)
                        stage(chunk + 1, 1 - b)
                        step = Chain(dve, s["step"], chunk * 5)
                        dve.wait_ge(s["rows"], chunk + 1)
                        for j in range(CH):
                            last = nc.vector.scalar_tensor_tensor(
                                same[:, j, :], rows_ps[b][:, j, :], key_st[:, b, j:j + 1], k.before[:, :],
                                ALU.is_equal, ALU.mult, accum_out=in_col[:, b, j:j + 1])
                        step(last)
                        dve.wait_ge(s["ranked"], chunk + 1)
                        step(nc.vector.tensor_tensor(picked[:, :, :], before_ps[b][:, :, :], one_d[:, b, :, :], ALU.mult))
                        step(nc.vector.tensor_reduce(before_col[:, :], picked[:, :, :], X, ALU.add))
                        step(nc.vector.tensor_tensor(rank[:, :], before_col[:, :], in_col[:, b, :], ALU.add))
                        nc.vector.tensor_scalar(k.spill[:, at], rank[:, :], float(k.CAP), None, ALU.is_ge)
                        nc.vector.tensor_scalar(over[:, :], rank[:, :], float(k.CAP), float(2 * k.SLOTS),
                                                ALU.is_ge, ALU.mult)
                        step(nc.vector.scalar_tensor_tensor(slot_f[:, :], k.key[:, at], float(P), rank[:, :],
                                                            ALU.mult, ALU.add))
                        dve.wait_ge(scattered[b], i * (16 * CH) + 16)
                        nc.vector.tensor_copy(place_st[:, b, :, :], k.place[:, at, :])
                        nc.vector.tensor_tensor(slot[:, b, :], slot_f[:, :], over[:, :], ALU.add)\
                            .then_inc(s["slots_ready"], 1)

                step = Chain(dve, s["step"], 2 * NPAIR * 5)
                normalise(k, s, step, nodes(k, k.res), nodes(k, k.cur), k.one)
                split3(k, step, k.table_s, nodes(k, k.cur), k.one)


def nodes(k, t):
    return t[:, :].rearrange("p (b d) -> p b d", d=k.D)


def split3(k, step, table, rows, rest):
    step(step.eng.tensor_copy(table[:, :, 0, :], rows))
    step(step.eng.tensor_tensor(rest, rows, table[:, :, 0, :], ALU.subtract))
    step(step.eng.tensor_copy(table[:, :, 1, :], rest))
    step(step.eng.tensor_tensor(table[:, :, 2, :], rest, table[:, :, 1, :], ALU.subtract))


def inverse_root(s, step, value, root, inv, tmp):
    dve = step.eng
    dve.wait_ge(s["root_ready"], 1)
    step(dve.reciprocal(inv, root))
    step(dve.tensor_tensor(tmp, inv, inv, ALU.mult))
    step(dve.tensor_tensor(tmp, tmp, value, ALU.mult))
    step(dve.tensor_scalar(tmp, tmp, -0.5, 1.5, ALU.mult, ALU.add))
    step(dve.tensor_tensor(inv, inv, tmp, ALU.mult))


def normalise(k, s, step, rows, h, centred):
    dve = step.eng
    shape = [P, k.NB, k.D]

    def wide(t):
        return t[:, :].unsqueeze(2).to_broadcast(shape)

    step(dve.tensor_reduce(k.mean[:, :], rows, X, ALU.add))
    step(dve.tensor_scalar(k.mean[:, :], k.mean[:, :], 1.0 / k.D, None, ALU.mult))
    step(dve.tensor_tensor(centred, rows, wide(k.mean), ALU.subtract))
    step(dve.tensor_tensor(h, centred, centred, ALU.mult))
    step(dve.tensor_reduce(k.var[:, :], h, X, ALU.add))
    dve.tensor_scalar(k.var[:, :], k.var[:, :], 1.0 / k.D, EPS_LN, ALU.mult, ALU.add).then_inc(s["value_ready"], 1)
    inverse_root(s, step, k.var[:, :], k.root[:, :], k.inv[:, :], k.mean[:, :])
    step(dve.tensor_tensor(centred, centred, wide(k.inv), ALU.mult))
    step(dve.tensor_scalar(h, centred, 0.0, None, ALU.max))


def sqrt_on_act(nc, k, s):
    def program(act):
        act.wait_ge(s["value_ready"], 1)
        nc.scalar.activation(k.root[:, :], k.var[:, :], ACT.Sqrt).then_inc(s["root_ready"], 1)
    return program


def idle(eng):
    pass


def count_spills(nc, k):
    spans = [(a, min(a + 512, k.NT)) for a in range(0, k.NT, 512)]
    with ExitStack() as st:
        col_ps = [st.enter_context(nc.psum_tensor(f"col_ps{i}", [P, 512], F32)) for i in range(len(spans))]
        all_f = st.enter_context(nc.sbuf_tensor("all_f", [1, len(spans)], F32))
        with phase(nc, "summed step") as (s, block):
            @block.tensor
            def _(pe):
                for i, (a, z) in enumerate(spans):
                    last = nc.tensor.matmul(col_ps[i][:, 0:z - a], k.ones[:, :], k.spill[:, a:z], start=True, stop=True)
                last.then_inc(s["summed"], 1)

            @block.vector
            def _(dve):
                step = Chain(dve, s["step"])
                dve.wait_ge(s["summed"], 1)
                for i, (a, z) in enumerate(spans):
                    dve.tensor_copy(k.col_spills[:, a:z], col_ps[i][0:1, 0:z - a])
                    last = dve.tensor_reduce(all_f[:, i:i + 1], col_ps[i][0:1, 0:z - a], X, ALU.add)
                step(last)
                with nc.allow_low_precision("whole numbers"):
                    step(dve.tensor_reduce(k.some_spill[:, :], all_f[:, :], X, ALU.max))


def spilled_edges(nc, k, stored, gathers, by, acc, width, stage):
    NB, D = k.NB, k.D
    group = max(g for g in range(1, NB + 1) if NB % g == 0 and g * width <= 512)
    n = NB // group
    spilled = nc.values_load(k.some_spill[0:1, 0:1], skip_runtime_bounds_check_because="only tested")
    with nc.If(spilled > 0):
        with spill_phase(nc, k) as (s, block):
            @block.sync
            def _(sp):
                for rows, table in stored:
                    sp.dma_start(table.rearrange("(b p) d -> p b d", p=P), rows).then_inc(s["spill_stored"], 16)
                sp.wait_ge(s["spill_stored"], 16 * len(stored))

            for engine in (block.gpsimd, block.tensor, block.scalar, block.vector):
                engine(idle)
        with nc.Fori(0, k.NT) as t:
            in_col = nc.values_load(k.col_spills[0:1, bass.ds(t, 1)], skip_runtime_bounds_check_because="only tested")
            with nc.If(in_col > 0):
                spilled_column(nc, k, t, gathers, by, acc, width, stage, group, n)
        nc.all_engine_barrier()


def spilled_column(nc, k, t, gathers, by, acc, width, stage, group, n):
    NB, D = k.NB, k.D
    with ExitStack() as st:
        def sb(name, shape, dt):
            return st.enter_context(nc.sbuf_tensor(name + "_" + stage, shape, dt))

        index = sb("sp_index", [P, 2], I32)
        ends = sb("sp_ends", [P, 2], I32)
        ends_f = sb("sp_ends_f", [P, 2], F32)
        place = sb("sp_place", [P, P], F32)
        block_hot = sb("sp_block", [P, NB], F32)
        row = sb("sp_row", [P, 2, D], F32)
        logit = sb("sp_logit", [P, 1], F32)
        spread = k.two if width > 1 else sb("sp_spread", [P, NB, 1], F32)
        total_ps = [st.enter_context(nc.psum_tensor(f"sp_ps{i}_{stage}", [P, group, width], F32)) for i in range(n)]
        with spill_phase(nc, k) as (s, block):
            block.sync(idle)

            @block.gpsimd
            def _(pool):
                pool.wait_ge(s["picked"], 1)
                for i, (table, _e) in enumerate(gathers):
                    pool.indirect_dma_start(out=row[:, i, :], out_offset=None, in_=table,
                                            in_offset=bass.IndirectOffsetOnAxis(ap=index[:, i:i + 1], axis=0),
                                            bounds_check=NB * P - 1, oob_is_err=False).then_inc(s["gathered_rows"], 16)

            @block.tensor
            def _(pe):
                pe.wait_ge(s["placed"], 1)
                for i in range(n):
                    last = pe.matmul(total_ps[i][:, :, :], place[:, :], spread[:, i * group:(i + 1) * group, :],
                                     start=True, stop=True)
                last.then_inc(s["multiplied"], 1)

            @block.scalar
            def _(act):
                if stage == "masks":
                    act.wait_ge(s["multiplied"], 1)
                    act.activation(logit[:, :], logit[:, :], ACT.Sigmoid, bias=k.b3[:, 0:1]).then_inc(s["multiplied"], 1)

            @block.vector
            def _(dve):
                step = Chain(dve, s["step"])
                edge = bass.ds(t, 1)
                for i, (_t, end) in enumerate(gathers):
                    last = dve.tensor_single_scalar(index[:, i:i + 1], end[:, edge], NB * P - 1, ALU.min)
                last.then_inc(s["picked"], 1)
                dve.tensor_single_scalar(ends[:, 0:1], by[:, edge], 7, ALU.logical_shift_right)
                step(dve.tensor_single_scalar(ends[:, 1:2], by[:, edge], P - 1, ALU.bitwise_and))
                step(dve.tensor_copy(ends_f[:, :], ends[:, :]))
                dve.tensor_scalar(place[:, :], k.iota[:, :], ends_f[:, 1:2], None, ALU.is_equal)
                step(dve.tensor_scalar(block_hot[:, :], k.iota[:, 0:NB], ends_f[:, 0:1], k.spill[:, edge],
                                       ALU.is_equal, ALU.mult))
                dve.wait_ge(s["gathered_rows"], 16 * len(gathers))
                summed = 1
                if stage == "masks":
                    step(dve.tensor_tensor(row[:, 0, :], row[:, 0, :], row[:, 1, :], ALU.add))
                    step(dve.scalar_tensor_tensor(row[:, 0, :], row[:, 0, :], 0.0, k.w3[:, :], ALU.max, ALU.mult))
                    dve.tensor_reduce(logit[:, :], row[:, 0, :], X, ALU.add).then_inc(s["multiplied"], 1)
                    dve.wait_ge(s["multiplied"], 2)
                    step(dve.tensor_scalar(logit[:, :], logit[:, :], ZETA - GAMMA, GAMMA, ALU.mult, ALU.add))
                    step(dve.tensor_scalar(logit[:, :], logit[:, :], 0.0, 1.0, ALU.max, ALU.min))
                    dve.tensor_copy(k.spill_mask[:, edge], logit[:, :])
                    step(dve.tensor_scalar(spread[:, :, 0], block_hot[:, :], logit[:, 0:1], None, ALU.mult))
                    summed = 3
                else:
                    if stage == "messages":
                        step(dve.tensor_tensor(block_hot[:, :], block_hot[:, :],
                                               k.spill_mask[:, edge].to_broadcast([P, NB]), ALU.mult))
                    step(dve.tensor_tensor(spread[:, :, :], block_hot[:, :].unsqueeze(2).to_broadcast([P, NB, D]),
                                           row[:, 0, :].unsqueeze(1).to_broadcast([P, NB, D]), ALU.mult))
                dve.sem_inc(s["placed"], 1)
                dve.wait_ge(s["multiplied"], summed)
                for i in range(n):
                    part, share = acc[:, i * group:(i + 1) * group, :], total_ps[i][:, :, :]
                    if stage == "messages":
                        wide = k.inv[:, i * group:(i + 1) * group].unsqueeze(2).to_broadcast([P, group, D])
                        step(dve.tensor_tensor(spread[:, i * group:(i + 1) * group, :], share, wide, ALU.mult))
                        share = spread[:, i * group:(i + 1) * group, :]
                    last = dve.tensor_tensor(part, part, share, ALU.add)
                step(last)


def build_and_sum(nc, k):
    NB, G, NG, D = k.NB, k.G, k.NG, k.D
    Q = NB * NG
    LOW = min(4, G)
    with ExitStack() as st:
        def sb(name, shape, dt):
            return st.enter_context(nc.sbuf_tensor(name, shape, dt))

        def ps(name, shape, dt=F32):
            return st.enter_context(nc.psum_tensor(name, shape, dt))

        places = sb("places", [P, NG, G * P, 2], U8)
        hot = sb("hot", [P, NG, 3, G * P], U8)
        hot_d = sb("hot_d", [P, 2, G, P], U8)
        counts = sb("counts", [P, 2, G, P], BF16)
        rows = sb("rows", [P, 2, PARTS * D], BF16)
        src_ps = ps("src_ps", [P, 8, P])
        dst_ps = ps("dst_ps", [P, 8, P])
        cnt_ps = ps("cnt_ps", [P, 8, P])
        sum_ps = ps("l0_ps", [P, G, D])
        sems = " ".join([f"places_in{g} stored{g}" for g in range(NG)])
        with phase(nc, "passed hotT src_turned dst_turned hot_ready hot_d_low hot_d_high counted counts_ready "
                       "rows_ready summed added step " + sems) as (s, block):
            places_in = [s[f"places_in{g}"] for g in range(NG)]
            stored = [s[f"stored{g}"] for g in range(NG)]

            @block.gpsimd
            def _(pool):
                def row(r, b, nth, first):
                    for g in range(NG):
                        if not first:
                            wait_count(pool, s, s["hotT"], (r - 1) * NG + g + 1)
                        tile = k.slots_dram[bass.ds((r * NB + g * G) * P, G * P), :]
                        pool.dma_start(places[:, g, :, :], tile.rearrange("a b -> (a b)").partition_broadcast(P))\
                            .then_inc(places_in[g], 16)
                each_row(pool, NB, row)

            @block.sync
            def _(sp):
                def row(r, b, nth, first):
                    for g in range(NG):
                        q = r * NG + g
                        wait_count(sp, s, s["hotT"], q + 1)
                        wait_count(sp, s, s["hot_ready"], q + 1)
                        sp.dma_start(k.hot_dram[bass.ds(r, 1), :, g, :, :].rearrange("r p a b -> (r p) a b"),
                                     hot[:, g, :, :]).then_inc(stored[g], 16)
                each_row(sp, NB, row)
                for g in range(NG):
                    sp.wait_ge(stored[g], 16 * NB)

            @block.tensor
            def _(pe):
                def turn(r, g, first):
                    q = r * NG + g
                    pe.wait_ge(s["hotT"], q + 1)
                    if not (first and g == 0):
                        pe.wait_ge(s["hot_ready"], q)
                    hold_waits(pe, s)
                    for j in range(G):
                        last = nc.tensor.matmul(src_ps[:, j, :], hot[:, g, 0, j * P:(j + 1) * P].bitcast(FP8),
                                                k.identb[:, :], start=True, stop=True)
                    last.then_inc(s["src_turned"], 1)
                    if not (first and g == 0):
                        pe.wait_ge(s["hot_d_low"], q)
                        pe.wait_ge(s["hot_d_high"], q)
                    hold_waits(pe, s)
                    for j in range(G):
                        last = nc.tensor.matmul(dst_ps[:, j, :], hot[:, g, 1, j * P:(j + 1) * P].bitcast(FP8),
                                                k.identb[:, :], start=True, stop=True)
                    last.then_inc(s["dst_turned"], 1)

                def count(q, g, b, first=False):
                    if not (first and g == 0):
                        pe.wait_ge(s["counts_ready"], q)
                    pe.wait_ge(s["hot_ready"], q + 1)
                    pe.wait_ge(s["hot_d_low"], q + 1)
                    pe.wait_ge(s["hot_d_high"], q + 1)
                    hold_waits(pe, s)
                    for j in range(G):
                        last = nc.tensor.matmul(cnt_ps[:, j, :], hot[:, g, 2, j * P:(j + 1) * P].bitcast(FP8),
                                                hot_d[:, (b + g) % 2, j, :].bitcast(FP8), start=True, stop=True)
                    last.then_inc(s["counted"], 1)

                def add_up(q, r, g, b):
                    pe.wait_ge(s["counts_ready"], q + 1)
                    pe.wait_ge(s["rows_ready"], r + 1)
                    pe.wait_ge(s["added"], q + 1)
                    for j in range(G):
                        for part in range(PARTS):
                            last = nc.tensor.matmul(sum_ps[:, j, :], counts[:, (b + g) % 2, j, :],
                                                    rows[:, b, part * D:(part + 1) * D],
                                                    start=part == 0, stop=part == PARTS - 1)
                    last.then_inc(s["summed"], 1)

                def row(r, b, nth, first):
                    for g in range(NG):
                        turn(r, g, first)
                        if g >= 1:
                            count(r * NG + g - 1, g - 1, b, first)
                        elif not first:
                            count(r * NG - 1, NG - 1, 1 - b)
                        if g >= 2:
                            add_up(r * NG + g - 2, r, g - 2, b)
                        elif not first:
                            add_up(r * NG + g - 2, r - 1, NG + g - 2, 1 - b)
                each_row(pe, NB, row)
                count(Q - 1, NG - 1, 0)
                add_up(Q - 2, NB - 1, NG - 2, 0)
                add_up(Q - 1, NB - 1, NG - 1, 0)

            @block.scalar
            def _(act):
                def take_dst_low(q, g, b):
                    act.wait_ge(s["dst_turned"], q + 1)
                    nc.scalar.activation(hot_d[:, (b + g) % 2, 0:LOW, :], dst_ps[:, 0:LOW, :], ACT.Copy,
                                         scale=float(HOT)).then_inc(s["hot_d_low"], 1)

                def take_counts(q, g, b):
                    act.wait_ge(s["counted"], q + 1)
                    nc.scalar.activation(counts[:, (b + g) % 2, :, :], cnt_ps[:, 0:G, :], ACT.Copy)\
                        .then_inc(s["counts_ready"], 1)

                def row(r, b, nth, first):
                    for g in range(NG):
                        act.wait_ge(s["src_turned"], r * NG + g + 1)
                        if not first:
                            act.wait_ge(stored[g], r * 16)
                        nc.scalar.activation(hot[:, g, 2, :].rearrange("p (j e) -> p j e", e=P), src_ps[:, 0:G, :],
                                             ACT.Copy, scale=float(HOT)).then_inc(s["hot_ready"], 1)
                        if g == 0:
                            nc.scalar.activation(rows[:, b, :].rearrange("p (a d) -> p a d", d=D),
                                                 k.table_s[:, bass.ds(r, 1), :, :].rearrange("p r a d -> p (r a) d"),
                                                 ACT.Copy).then_inc(s["rows_ready"], 1)
                        take_dst_low(r * NG + g, g, b)
                        if g >= 1:
                            take_counts(r * NG + g - 1, g - 1, b)
                        elif not first:
                            take_counts(r * NG - 1, NG - 1, 1 - b)
                each_row(act, NB, row)
                take_counts(Q - 1, NG - 1, 0)

            @block.vector
            def _(dve):
                sums = k.one
                dve.memset(k.one, 0.0).then_inc(s["added"], 1)
                dve.wait_ge(s["added"], 1)

                def take_dst_high(q, g, b):
                    dve.wait_ge(s["dst_turned"], q + 1)
                    dve.tensor_scalar(hot_d[:, (b + g) % 2, LOW:G, :], dst_ps[:, LOW:G, :], float(HOT), None, ALU.mult)\
                        .then_inc(s["hot_d_high"], 1)

                def add_in(q, g):
                    dve.wait_ge(s["summed"], q + 1)
                    dve.tensor_tensor(sums[:, g * G:(g + 1) * G, :], sums[:, g * G:(g + 1) * G, :], sum_ps[:, :, :],
                                      ALU.add).then_inc(s["added"], 1)

                def row(r, b, nth, first):
                    for g in range(NG):
                        dve.wait_ge(places_in[g], r * 16 + 16)
                        if not first:
                            dve.wait_ge(stored[g], r * 16)
                        dve.tensor_scalar(hot[:, g, 0:2, :], places[:, g, :, :].rearrange("p s e -> p e s"), k.pcol[:, 0:1],
                                          float(HOT), ALU.is_equal, ALU.mult).then_inc(s["hotT"], 1)
                        if g >= 1:
                            take_dst_high(r * NG + g - 1, g - 1, b)
                        elif not first:
                            take_dst_high(r * NG - 1, NG - 1, 1 - b)
                        if g >= 3:
                            add_in(r * NG + g - 3, g - 3)
                        elif not first:
                            add_in(r * NG + g - 3, NG + g - 3)
                each_row(dve, NB, row)
                take_dst_high(Q - 1, NG - 1, 0)
                for back in (3, 2, 1):
                    add_in(Q - back, NG - back)
                dve.wait_ge(s["added"], Q + 1)


def second_table(nc, k):
    with phase(nc, "value_ready root_ready step") as (s, block):
        block.scalar(sqrt_on_act(nc, k, s))

        @block.vector
        def _(dve):
            step = Chain(dve, s["step"])
            step(dve.tensor_tensor(nodes(k, k.res), nodes(k, k.res), k.one, ALU.add))
            normalise(k, s, step, nodes(k, k.res), nodes(k, k.cur), k.one)


def allocate_layers(nc, k, st):
    def sb(name, shape, dt):
        return st.enter_context(nc.sbuf_tensor(name, shape, dt))

    k.w1 = sb("w1", [k.D, 2 * k.D], F32)
    k.b1 = sb("b1", [2 * k.D, 1], F32)
    k.w2 = sb("w2", [2 * k.D, 2 * k.D], F32)
    k.b2 = sb("b2", [P, 2 * k.D], F32)
    k.w3 = sb("w3", [P, k.D], F32)
    k.b3 = sb("b3", [P, 1], F32)
    k.mask = sb("mask", [P, k.NB * k.NB], F32)
    k.sums = sb("sums", [P, k.NB], F32)


def node_products(nc, k, l, w):
    D, NB, BLK = k.D, k.NB, 4
    spans = [(a, min(a + BLK, NB)) for a in range(0, NB, BLK)]
    n = len(spans)
    with ExitStack() as st:
        def sb(name, shape, dt):
            return st.enter_context(nc.sbuf_tensor(name, shape, dt))

        def ps(name, shape, dt=F32):
            return st.enter_context(nc.psum_tensor(name, shape, dt))

        curT = sb("curT", [D, 2, BLK * P], F32)
        hid = sb("hid", [2 * D, 2, BLK * P], F32)
        rest = sb("rest", [P, 4, BLK, 2 * D], F32)
        turn_ps = [ps(f"turn_ps{i}", [D, BLK * P]) for i in range(2)]
        hid_ps = [ps(f"hid_ps{i}", [2 * D, BLK * P]) for i in range(2)]
        att_ps = [ps(f"att_ps{i}", [P, BLK, 2 * D]) for i in range(2)]
        with phase(nc, "cleared weights turned curT_ready hidden hid_ready attended taken "
                       "first_ready rest_ready second_ready third_ready res_added", again=True) as (s, block):
            @block.sync
            def _(sp):
                def col(a):
                    return a[bass.ds(l, 1), :].rearrange("o d -> d o")

                at = bass.ds(l, 1)
                loads = [
                    (k.w1[:, 0:D], w.nb_w[at, :, :].rearrange("o a b -> (o a) b")),
                    (k.w1[:, D:2 * D], w.self_w[at, :, :].rearrange("o a b -> (o a) b")),
                    (k.b1[0:D, :], col(w.nb_b)), (k.b1[D:2 * D, :], col(w.self_b)),
                    (k.b2[:, D:2 * D], w.att1_b[at, :].rearrange("o d -> (o d)").partition_broadcast(P)),
                    (k.w3[:, :], w.att2_w[at, :, :].rearrange("o d x -> (o d x)").partition_broadcast(P)),
                    (k.b3[:, :], w.att2_b[at, :].rearrange("o x -> (o x)").partition_broadcast(P)),
                ]
                for dst, src in loads:
                    sp.dma_start(dst, src).then_inc(s["weights"], 16)
                sp.wait_ge(s["cleared"], 1)
                for h in range(2):
                    sp.dma_start(k.w2[h * D:(h + 1) * D, h * D:(h + 1) * D],
                                 w.att1_w[at, h * D:(h + 1) * D, :].rearrange("o a b -> (o a) b"))\
                        .then_inc(s["weights"], 16)

            @block.tensor
            def _(pe):
                cur = nodes(k, k.cur)

                def turn(m):
                    a, z = spans[m]
                    if m >= 2:
                        pe.wait_ge(s["curT_ready"], m - 1)
                    for blk in range(a, z):
                        last = nc.tensor.transpose(turn_ps[m % 2][:, (blk - a) * P:(blk - a + 1) * P],
                                                   cur[:, blk, :], k.ident[:, :])
                    last.then_inc(s["turned"], 1)

                def hide(m):
                    a, z = spans[m]
                    pe.wait_ge(s["curT_ready"], m + 1)
                    if m >= 2:
                        pe.wait_ge(s["hid_ready"], m - 1)
                    nc.tensor.matmul(hid_ps[m % 2][:, 0:(z - a) * P], k.w1[:, :], curT[:, m % 2, 0:(z - a) * P],
                                     start=True, stop=True).then_inc(s["hidden"], 1)

                def attend(m):
                    a, z = spans[m]
                    pe.wait_ge(s["hid_ready"], m + 1)
                    if m >= 2:
                        pe.wait_ge(s["taken"], m - 1)
                    for j in range(z - a):
                        last = nc.tensor.matmul(att_ps[m % 2][:, j, :], hid[:, m % 2, j * P:(j + 1) * P], k.w2[:, :],
                                                start=True, stop=True)
                    last.then_inc(s["attended"], 1)

                pe.wait_ge(s["weights"], 16 * 9)
                for m in range(n + 2):
                    if m < n:
                        turn(m)
                    if 0 <= m - 1 < n:
                        hide(m - 1)
                    if m >= 2:
                        attend(m - 2)

            @block.scalar
            def _(act):
                act.wait_ge(s["weights"], 16 * 9)

                def relu(m):
                    a, z = spans[m]
                    act.wait_ge(s["hidden"], m + 1)
                    if m >= 2:
                        act.wait_ge(s["attended"], m - 1)
                    nc.scalar.activation(hid[:, m % 2, 0:(z - a) * P], hid_ps[m % 2][:, 0:(z - a) * P], ACT.Relu,
                                         bias=k.b1[:, 0:1]).then_inc(s["hid_ready"], 1)

                for m in range(n + 1):
                    if m < n:
                        a, z = spans[m]
                        act.wait_ge(s["turned"], m + 1)
                        if m >= 2:
                            act.wait_ge(s["hidden"], m - 1)
                        nc.scalar.activation(curT[:, m % 2, 0:(z - a) * P], turn_ps[m % 2][:, 0:(z - a) * P],
                                             ACT.Copy).then_inc(s["curT_ready"], 1)
                    if m >= 1:
                        relu(m - 1)

            @block.gpsimd
            def _(pool):
                pool.tensor_tensor(k.res[:, :], k.res[:, :], k.cur[:, :], ALU.add).then_inc(s["res_added"], 1)
                for m, (a, z) in enumerate(spans):
                    pool.wait_ge(s["first_ready"], m + 1)
                    if m >= 4:
                        pool.wait_ge(s["third_ready"], m - 3)
                    pool.tensor_tensor(rest[:, m % 4, 0:z - a, :], k.both[:, a:z, :], k.table[:, a:z, 0, :],
                                       ALU.subtract).then_inc(s["rest_ready"], 1)
                pool.wait_ge(s["res_added"], 1)

            @block.vector
            def _(dve):
                dve.memset(k.b2[:, 0:D], 0.0)
                dve.memset(k.w2[:, :], 0.0).then_inc(s["cleared"], 1)
                dve.wait_ge(s["cleared"], 1)
                dve.wait_ge(s["weights"], 16 * 9)
                for m in range(n + 1):
                    if m < n:
                        a, z = spans[m]
                        dve.wait_ge(s["attended"], m + 1)
                        dve.tensor_tensor(k.both[:, a:z, :], att_ps[m % 2][:, 0:z - a, :],
                                          k.b2[:, :].unsqueeze(1).to_broadcast([P, z - a, 2 * D]), ALU.add)\
                            .then_inc(s["taken"], 1)
                    if m >= 1:
                        u, v = spans[m - 1]
                        left = rest[:, (m - 1) % 4, 0:v - u, :]
                        dve.wait_ge(s["rest_ready"], m)
                        dve.tensor_copy(k.table[:, u:v, 1, :], left).then_inc(s["second_ready"], 1)
                    if m < n:
                        dve.wait_ge(s["taken"], m + 1)
                        dve.tensor_copy(k.table[:, a:z, 0, :], k.both[:, a:z, :]).then_inc(s["first_ready"], 1)
                    if m >= 1:
                        dve.wait_ge(s["second_ready"], m)
                        dve.tensor_tensor(k.table[:, u:v, 2, :], left, k.table[:, u:v, 1, :], ALU.subtract)\
                            .then_inc(s["third_ready"], 1)
                dve.wait_ge(s["third_ready"], n)


def edge_masks(nc, k):
    NB, G, NG, D = k.NB, k.G, k.NG, k.D
    SUMS_AT = max(0, NG - 2)
    with ExitStack() as st:
        def sb(name, shape, dt):
            return st.enter_context(nc.sbuf_tensor(name, shape, dt))

        def ps(name, shape, dt=F32):
            return st.enter_context(nc.psum_tensor(name, shape, dt))

        hotT = sb("hotT_a", [P, 2, NG, 2, G * P], U8)
        hot = sb("hot_a", [P, 2, NG, G * P], U8)
        rows = sb("rows_a", [P, 2, PARTS * D], BF16)
        weighed = sb("weighed", [P, 2, G, D], F32)
        logit = sb("logit", [P, 2, NB], F32)
        gate = sb("gate", [P, 2, NB], F32)
        fresh = sb("fresh", [P, NB], F32)
        parts = sb("parts", [P, NB, PARTS], BF16)
        pre_ps = [ps(f"pre_ps{g}", [P, 8, D]) for g in range(NG)]
        total_ps = ps("total_ps", [P, 512])
        sems = " ".join([f"in{b}_{g}" for b in range(2) for g in range(NG)] + ["src_in0", "src_in1"])
        with phase(nc, "passed rows_ready gathered weigh logits gated parts_ready summed taken step pool_step "
                       + sems, again=True) as (s, block):
            loaded = [[s[f"in{b}_{g}"] for g in range(NG)] for b in range(2)]
            src_loaded = [s["src_in0"], s["src_in1"]]

            @block.sync
            def _(sp):
                def row(r, b, nth, first):
                    tiles = k.hot_dram[bass.ds(r, 1), :, :, :, :].rearrange("r p g a b -> (r p) g a b")
                    for g in range(NG):
                        if not first:
                            wait_count(sp, s, s["gathered"], (r - 1) * NG + g + 1)
                        sp.dma_start(hotT[:, b, g, :, :], tiles[:, g, 0:2, :]).then_inc(loaded[b][g], 16)
                    wait_count(sp, s, s["summed"], r + 1)
                    sp.dma_start(hot[:, b, :, :], tiles[:, :, 2, :]).then_inc(src_loaded[b], 16)
                each_row(sp, NB, row)

            @block.tensor
            def _(pe):
                pe.sem_inc(s["summed"], 2)
                pe.sem_inc(s["gathered"], NG)

                def gather(q, r, g, b, nth):
                    pe.wait_ge(loaded[b][g], nth * 16)
                    pe.wait_ge(s["weigh"], q + 1)
                    if g == 0:
                        pe.wait_ge(s["rows_ready"], r + 1)
                    hold_waits(pe, s)
                    for j in range(G):
                        d = (g * G + j)
                        for end in range(2):
                            for part in range(PARTS):
                                table = rows[:, b, part * D:(part + 1) * D] if end == 0 else k.table_d[:, d, part, :]
                                last = nc.tensor.matmul(pre_ps[g][:, j, :],
                                                        hotT[:, b, g, end, j * P:(j + 1) * P].bitcast(FP8),
                                                        table, start=end + part == 0, stop=end == 1 and part == 2)
                    last.then_inc(s["gathered"], 1)

                def sum_masks(r, b, nth):
                    pe.wait_ge(src_loaded[b], nth * 16)
                    pe.wait_ge(s["parts_ready"], r + 1)
                    pe.wait_ge(s["taken"], r + 1)
                    hold_waits(pe, s)
                    for g in range(NG):
                        for j in range(G):
                            t = g * G + j
                            last = nc.tensor.matmul(total_ps[:, 0:PARTS], hot[:, b, g, j * P:(j + 1) * P].bitcast(FP8),
                                                    parts[:, t, :], start=t == 0, stop=t == NB - 1)
                    last.then_inc(s["summed"], 1)

                def row(r, b, nth, first):
                    for g in range(NG):
                        gather(r * NG + g, r, g, b, nth)
                        if g == SUMS_AT and not first:
                            sum_masks(r - 1, 1 - b, nth if b == 1 else nth - 1)
                each_row(pe, NB, row)
                sum_masks(NB - 1, 0, NB // 2 + 1)

            @block.scalar
            def _(act):
                def gates(r, b):
                    act.wait_ge(s["logits"], r * NG + NG)
                    nc.scalar.activation(gate[:, b, :], logit[:, b, :], ACT.Sigmoid, bias=k.b3[:, 0:1])\
                        .then_inc(s["gated"], 1)

                def row(r, b, nth, first):
                    if not first:
                        act.wait_ge(s["gathered"], r * NG)
                    nc.scalar.activation(rows[:, b, :].rearrange("p (a d) -> p a d", d=D),
                                         k.table_s[:, bass.ds(r, 1), :, :].rearrange("p r a d -> p (r a) d"),
                                         ACT.Copy).then_inc(s["rows_ready"], 1)
                    if not first:
                        gates(r - 1, 1 - b)
                each_row(act, NB, row)
                gates(NB - 1, 0)

            @block.gpsimd
            def _(pool):
                def row(r, b, nth, first):
                    pool.sem_clear(s["pool_step"])
                    step = Chain(pool, s["pool_step"])
                    wait_count(pool, s, s["gated"], r + 1)
                    step(pool.tensor_scalar(fresh[:, :], gate[:, b, :], ZETA - GAMMA, GAMMA, ALU.mult, ALU.add))
                    step(pool.tensor_scalar(fresh[:, :], fresh[:, :], 0.0, 1.0, ALU.max, ALU.min))
                    pool.tensor_copy(k.mask[:, bass.ds(r * NB, NB)], fresh[:, :])
                    step(pool.tensor_copy(parts[:, :, 0], fresh[:, :]))
                    step(pool.tensor_tensor(fresh[:, :], fresh[:, :], parts[:, :, 0], ALU.subtract))
                    step(pool.tensor_copy(parts[:, :, 1], fresh[:, :]))
                    step(pool.tensor_tensor(fresh[:, :], fresh[:, :], parts[:, :, 1], ALU.subtract))
                    step(pool.tensor_copy(parts[:, :, 2], fresh[:, :]))
                    pool.sem_inc(s["parts_ready"], 1)
                each_row(pool, NB, row)

            @block.vector
            def _(dve):
                dve.sem_inc(s["weigh"], NG)
                dve.sem_inc(s["taken"], 1)

                def reduce(q, g, b):
                    dve.wait_ge(s["weigh"], q + NG + 1)
                    dve.tensor_reduce(logit[:, b, g * G:(g + 1) * G], weighed[:, (b + g) % 2, :, :], X, ALU.add)\
                        .then_inc(s["logits"], 1)

                def take(r, b):
                    dve.wait_ge(s["summed"], r + 3)
                    dve.tensor_reduce(k.sums[:, bass.ds(r, 1)], total_ps[:, 0:PARTS], X, ALU.add).then_inc(s["taken"], 1)

                def row(r, b, nth, first):
                    for g in range(NG):
                        q = r * NG + g
                        if not (first and g < 2):
                            dve.wait_ge(s["logits"], q - 1)
                        dve.wait_ge(s["gathered"], q + NG + 1)
                        dve.scalar_tensor_tensor(weighed[:, (b + g) % 2, :, :], pre_ps[g][:, 0:G, :], 0.0,
                                                 k.w3[:, :].unsqueeze(1).to_broadcast([P, G, D]),
                                                 ALU.max, ALU.mult).then_inc(s["weigh"], 1)
                        if g >= 1:
                            reduce(q - 1, g - 1, b)
                        elif not first:
                            reduce(q - 1, NG - 1, 1 - b)
                    if not first:
                        take(r - 1, 1 - b)
                each_row(dve, NB, row)
                reduce(NB * NG - 1, NG - 1, 0)
                take(NB - 1, 0)
                dve.wait_ge(s["taken"], NB + 1)


def scale_rows(nc, k):
    with phase(nc, "value_ready root_ready step", again=True) as (s, block):
        block.scalar(sqrt_on_act(nc, k, s))

        @block.vector
        def _(dve):
            step = Chain(dve, s["step"])
            dve.tensor_scalar(k.var[:, :], k.sums[:, :], EPS_SUM, None, ALU.add).then_inc(s["value_ready"], 1)
            inverse_root(s, step, k.var[:, :], k.root[:, :], k.inv[:, :], k.mean[:, :])
            step(dve.tensor_scalar(k.inv[:, :], k.inv[:, :], 0.0, D_MAX, ALU.max, ALU.min))
            step(dve.tensor_tensor(k.one, nodes(k, k.cur),
                                   k.inv[:, :].unsqueeze(2).to_broadcast([P, k.NB, k.D]), ALU.mult))
            split3(k, step, k.table_d, k.one, k.two)


def sum_messages(nc, k):
    NB, G, NG, D = k.NB, k.G, k.NG, k.D
    Q = NB * NG
    LATE = min(4, NG - 1)
    with ExitStack() as st:
        def sb(name, shape, dt):
            return st.enter_context(nc.sbuf_tensor(name, shape, dt))

        def ps(name, shape, dt=F32):
            return st.enter_context(nc.psum_tensor(name, shape, dt))

        hot = sb("hot_b", [P, 2, NG, 2, G * P], U8)
        message = sb("message", [P, NG, G, D], F32)
        total = sb("total", [P, 2, D], F32)
        parts = sb("message_parts", [P, NG, G, PARTS, D], BF16)
        row_ps = [ps(f"row_ps{i}", [P, 8, D]) for i in range(4)]
        sum_ps = [ps(f"sum_ps{i}", [P, PARTS * D]) for i in range(2)]
        sems = " ".join([f"in{b}_{g}" for b in range(2) for g in range(NG)])
        with phase(nc, "passed gathered scaled first_ready rest_ready second_ready third_ready added taken row_done "
                       + sems, again=True) as (s, block):
            loaded = [[s[f"in{b}_{g}"] for g in range(NG)] for b in range(2)]

            def late(r, g, b, by, first, do):
                if g >= by:
                    do(r * NG + g - by, r, g - by, b)
                elif not first:
                    do(r * NG + g - by, r - 1, NG + g - by, 1 - b)

            @block.sync
            def _(sp):
                def row(r, b, nth, first):
                    for g in range(NG):
                        if not first:
                            wait_count(sp, s, s["added"], (r - 1) * NG + g + 1)
                        sp.dma_start(hot[:, b, g, :, :],
                                     k.hot_dram[bass.ds(r, 1), :, g, 1:3, :].rearrange("r p a b -> (r p) a b"))\
                            .then_inc(loaded[b][g], 16)
                each_row(sp, NB, row)

            @block.tensor
            def _(pe):
                pe.sem_inc(s["added"], NG)

                def gather(q, r, g, b, nth):
                    pe.wait_ge(loaded[b][g], nth * 16)
                    pe.wait_ge(s["scaled"], q + 1)
                    hold_waits(pe, s)
                    for j in range(G):
                        for part in range(PARTS):
                            last = nc.tensor.matmul(row_ps[g % 4][:, j, :],
                                                    hot[:, b, g, 0, j * P:(j + 1) * P].bitcast(FP8),
                                                    k.table_d[:, g * G + j, part, :],
                                                    start=part == 0, stop=part == PARTS - 1)
                    last.then_inc(s["gathered"], 1)

                def add_up(q, r, g, b):
                    pe.wait_ge(s["third_ready"], q + 1)
                    if g == 0:
                        pe.wait_ge(s["taken"], r + 1)
                    hold_waits(pe, s)
                    for j in range(G):
                        t = g * G + j
                        last = nc.tensor.matmul(sum_ps[b][:, :],
                                                hot[:, b, g, 1, j * P:(j + 1) * P].bitcast(FP8),
                                                parts[:, g, j, :, :].rearrange("p c d -> p (c d)"),
                                                start=t == 0, stop=t == NB - 1)
                    last.then_inc(s["added"], 1)

                def row(r, b, nth, first):
                    for g in range(NG):
                        gather(r * NG + g, r, g, b, nth)
                        late(r, g, b, LATE, first, add_up)
                each_row(pe, NB, row)
                for back in range(LATE, 0, -1):
                    add_up(Q - back, NB - 1, NG - back, 0)

            @block.scalar
            def _(act):
                act.sem_inc(s["row_done"], 2)

                def finish(r, b):
                    act.wait_ge(s["taken"], r + 3)
                    nc.scalar.activation(k.cur[:, bass.ds(r * D, D)], total[:, b, :], ACT.Copy,
                                         scale=k.inv[:, bass.ds(r, 1)])\
                        .then_inc(s["row_done"], 1)

                def second(q, r, g, b):
                    act.wait_ge(s["rest_ready"], q + 1)
                    nc.scalar.activation(parts[:, g, :, 1, :], message[:, g, :, :], ACT.Copy)\
                        .then_inc(s["second_ready"], 1)

                def row(r, b, nth, first):
                    for g in range(NG):
                        q = r * NG + g
                        act.wait_ge(s["scaled"], q + 4)
                        if not first:
                            act.wait_ge(s["added"], q + 1)
                        nc.scalar.activation(parts[:, g, :, 0, :], message[:, g, :, :], ACT.Copy)\
                            .then_inc(s["first_ready"], 1)
                        late(r, g, b, 1, first, second)
                    if not first:
                        finish(r - 1, 1 - b)
                each_row(act, NB, row)
                second(Q - 1, NB - 1, NG - 1, 0)
                finish(NB - 1, 0)
                act.wait_ge(s["row_done"], NB + 2)

            @block.gpsimd
            def _(pool):
                def row(r, b, nth, first):
                    for g in range(NG):
                        pool.wait_ge(s["first_ready"], r * NG + g + 1)
                        pool.tensor_tensor(message[:, g, :, :], message[:, g, :, :], parts[:, g, :, 0, :],
                                           ALU.subtract).then_inc(s["rest_ready"], 1)
                each_row(pool, NB, row)

            @block.vector
            def _(dve):
                dve.sem_inc(s["scaled"], 3)
                dve.sem_inc(s["taken"], 2)

                def third(q, r, g, b):
                    dve.wait_ge(s["second_ready"], q + 1)
                    dve.tensor_tensor(parts[:, g, :, 2, :], message[:, g, :, :], parts[:, g, :, 1, :],
                                      ALU.subtract).then_inc(s["third_ready"], 1)

                def take(r, b):
                    dve.wait_ge(s["row_done"], r + 1)
                    dve.wait_ge(s["added"], (r + 1) * NG + NG)
                    dve.tensor_reduce(total[:, b, :], sum_ps[b][:, :].rearrange("p (c d) -> p d c", d=D), X, ALU.add)\
                        .then_inc(s["taken"], 1)

                def row(r, b, nth, first):
                    for g in range(NG):
                        q = r * NG + g
                        dve.wait_ge(s["gathered"], q + 1)
                        if not first:
                            dve.wait_ge(s["third_ready"], q - NG + 1)
                        dve.tensor_tensor(message[:, g, :, :], row_ps[g % 4][:, 0:G, :],
                                          k.mask[:, bass.ds(r * NB + g * G, G)].unsqueeze(2).to_broadcast([P, G, D]),
                                          ALU.mult).then_inc(s["scaled"], 1)
                        late(r, g, b, 2, first, third)
                        if g == min(5, NG - 1) and not first:
                            take(r - 1, 1 - b)
                each_row(dve, NB, row)
                third(Q - 2, NB - 1, NG - 2, 0)
                third(Q - 1, NB - 1, NG - 1, 0)
                take(NB - 1, 0)


def store(nc, k, out):
    whole = k.N // P
    with phase(nc, "stored summed") as (s, block):
        @block.vector
        def _(dve):
            dve.tensor_tensor(k.res[:, :], k.res[:, :], k.cur[:, :], ALU.add).then_inc(s["summed"], 1)

        @block.sync
        def _(sp):
            sp.wait_ge(s["summed"], 1)
            sp.dma_start(out[0:whole * P, :].rearrange("(b p) d -> p b d", p=P),
                         nodes(k, k.res)[:, 0:whole, :]).then_inc(s["stored"], 16)
            if k.N > whole * P:
                sp.dma_start(out[whole * P:k.N, :], nodes(k, k.res)[0:k.N - whole * P, whole, :]).then_inc(s["stored"], 16)
            sp.wait_ge(s["stored"], 16 * (1 + (k.N > whole * P)))


def gnn(nc, x, src, dst, nb_w, nb_b, self_w, self_b, att1_w, att1_b, att2_w, att2_b, out, cap=P):
    k = make_plan(x, src, dst, nb_w, out, cap)
    w = Record()
    w.nb_w, w.nb_b, w.self_w, w.self_b = nb_w, nb_b, self_w, self_b
    w.att1_w, w.att1_b, w.att2_w, w.att2_b = att1_w, att1_b, att2_w, att2_b
    k.slots_dram = nc.dram_tensor("slots_scratch", [k.SLOTS, 2], U8).ap()
    k.hot_dram = nc.dram_tensor("hot_scratch", [k.NB, P, k.NG, 3, k.G * P], U8).ap()
    k.rows_a_dram = nc.dram_tensor("rows_a_scratch", [k.NB * P, k.D], F32).ap()
    k.rows_b_dram = nc.dram_tensor("rows_b_scratch", [k.NB * P, k.D], F32).ap()
    with ExitStack() as st:
        allocate(nc, k, st)
        with ExitStack() as sort_st:
            allocate_sort(nc, k, sort_st)
            constants(nc, k)
            load_inputs(nc, k, src, dst, x)
            sort_edges(nc, k)
        count_spills(nc, k)
        build_and_sum(nc, k)
        spilled_edges(nc, k, [(nodes(k, k.cur), k.rows_a_dram)], [(k.rows_a_dram, k.srci)], k.dsti, k.one, k.D, "hop")
        second_table(nc, k)
        allocate_layers(nc, k, st)
        with nc.Fori(0, k.L) as l:
            node_products(nc, k, l, w)
            edge_masks(nc, k)
            spilled_edges(nc, k, [(k.one, k.rows_a_dram), (k.two, k.rows_b_dram)],
                          [(k.rows_a_dram, k.srci), (k.rows_b_dram, k.dsti)], k.srci,
                          k.sums[:, :].unsqueeze(2), 1, "masks")
            scale_rows(nc, k)
            sum_messages(nc, k)
            spilled_edges(nc, k, [(k.one, k.rows_a_dram)], [(k.rows_a_dram, k.dsti)], k.srci,
                          nodes(k, k.cur), k.D, "messages")
        store(nc, k, out)


_INS = ["x", "src", "dst", "L1_gnn_nb_W", "L1_gnn_nb_b", "L1_gnn_self_W", "L1_gnn_self_b",
        "L1_gnn_att1_W", "L1_gnn_att1_b", "L1_gnn_att2_W", "L1_gnn_att2_b"]


def kernel(**inputs):
    import numpy as _np
    import concourse.bacc as _bacc
    from concourse import mybir as _mybir
    from concourse.bass_utils import run_bass_kernel_spmd as _run

    nc = _bacc.Bacc("TRN2", target_bir_lowering=False, num_devices=1)
    arrays, args = {}, []
    for name in _INS:
        a = _np.ascontiguousarray(inputs[name])
        arrays[f"in_{name}"] = a
        args.append(nc.dram_tensor(f"in_{name}", a.shape, _mybir.dt.from_np(a.dtype), kind="ExternalInput").ap())
    shape = inputs["x"].shape
    args.append(nc.dram_tensor("out_0", shape, _mybir.dt.float32, kind="ExternalOutput").ap())
    gnn(nc, *args)
    r = _run(nc, [arrays], core_ids=[0])
    return r.results[0]["out_0"]
```
